# Optimizing a Trainium2 kernel written in Bass

```python
import numpy as np
import jax
import jax.numpy as jnp

def _softmax(x, axis=-1):
    return jax.nn.softmax(x, axis=axis)

def _gelu(x):
    return jax.nn.gelu(x, approximate=True)

def _silu(x):
    return jax.nn.silu(x)

def _sigmoid(x):
    return jax.nn.sigmoid(x)

def _layernorm(x, axis=-1, eps=1e-05):
    m = jnp.mean(x, axis=axis, keepdims=True)
    v = jnp.var(x, axis=axis, keepdims=True)
    return (x - m) / jnp.sqrt(v + eps)

def _scatter_add(tgt, idx, src, axis=0):
    return tgt.at[idx].add(src)

def _segment_sum(src, seg, n):
    return jax.ops.segment_sum(src, seg, n)
kernel_name = 'mk_recurrent_d1_jaxref_r8_3d9e85'

def setup_inputs(seed: int=0):
    np.random.seed(seed)
    _w = jnp.asarray

    def _L0_attn_setup():
        import jax, jax.numpy as jnp
        import numpy as np
        from jax import lax
        D_MODEL = 128
        D_STATE = 64
        D_CONV = 4
        EXPAND = 2
        D_INNER = D_MODEL * EXPAND
        BATCH = 2
        T = 128
        EPS = 1e-05
        key = jax.random.key(seed)
        ks = jax.random.split(key, 8)
        s = 0.02
        return {'x': jax.random.normal(ks[0], (BATCH, T, D_MODEL), jnp.float32), 'norm_w': jnp.ones((D_MODEL,), jnp.float32), 'norm_b': jnp.zeros((D_MODEL,), jnp.float32), 'Win': jax.random.normal(ks[1], (D_MODEL, 2 * D_INNER), jnp.float32) * s, 'conv_w': jax.random.normal(ks[2], (D_INNER, 1, D_CONV), jnp.float32) * s, 'conv_b': jnp.zeros((D_INNER,), jnp.float32), 'dt_w': jax.random.normal(ks[3], (D_INNER, D_INNER), jnp.float32) * s, 'dt_b': jnp.zeros((D_INNER,), jnp.float32), 'A_log': jnp.broadcast_to(jnp.log(jnp.arange(1, D_STATE + 1, dtype=jnp.float32))[None, :], (D_INNER, D_STATE)).copy(), 'D': jnp.ones((D_INNER,), jnp.float32), 'Bp': jax.random.normal(ks[4], (D_INNER, D_STATE), jnp.float32) * s, 'Cp': jax.random.normal(ks[5], (D_INNER, D_STATE), jnp.float32) * s, 'Wout': jax.random.normal(ks[6], (D_INNER, D_MODEL), jnp.float32) * s}
    _L0_attn_in = _L0_attn_setup()

    def _L0_ffn_setup():
        import jax, jax.numpy as jnp
        import numpy as np
        B, T, C = (2, 128, 128)
        H = 512
        E_R, E_S, K = (8, 2, 2)

        def _rmsnorm(x, g):
            eps = jnp.finfo(x.dtype).eps
            return x * jax.lax.rsqrt(jnp.mean(x * x, axis=-1, keepdims=True) + eps) * g

        def _experts_mlp(x, g, W1, b1, W2, b2):
            xn = _rmsnorm(x, g)
            h = jnp.einsum('btc,ech->bteh', xn, W1) + b1
            h = jax.nn.gelu(h, approximate=False)
            return jnp.einsum('bteh,ehc->btec', h, W2) + b2
        key = jax.random.key(seed)
        ks = jax.random.split(key, 12)
        s = 0.02
        return {'u': jax.random.normal(ks[0], (B, T, C), dtype=jnp.float32), 'g_shared': jnp.ones((C,), jnp.float32), 'W1_s': jax.random.normal(ks[1], (E_S, C, H), jnp.float32) * s, 'b1_s': jax.random.normal(ks[2], (E_S, H), jnp.float32) * s, 'W2_s': jax.random.normal(ks[3], (E_S, H, C), jnp.float32) * s, 'b2_s': jax.random.normal(ks[4], (E_S, C), jnp.float32) * s, 'g_routed': jnp.ones((C,), jnp.float32), 'W1_r': jax.random.normal(ks[5], (E_R, C, H), jnp.float32) * s, 'b1_r': jax.random.normal(ks[6], (E_R, H), jnp.float32) * s, 'W2_r': jax.random.normal(ks[7], (E_R, H, C), jnp.float32) * s, 'b2_r': jax.random.normal(ks[8], (E_R, C), jnp.float32) * s, 'centroids': jax.random.normal(ks[9], (C, E_R), jnp.float32) * s}
    _L0_ffn_in = _L0_ffn_setup()
    _d = {'L0_attn_x': _L0_attn_in['x'], 'L0_attn_norm_w': _L0_attn_in['norm_w'], 'L0_attn_norm_b': _L0_attn_in['norm_b'], 'L0_attn_Win': _L0_attn_in['Win'], 'L0_attn_conv_w': _L0_attn_in['conv_w'], 'L0_attn_conv_b': _L0_attn_in['conv_b'], 'L0_attn_dt_w': _L0_attn_in['dt_w'], 'L0_attn_dt_b': _L0_attn_in['dt_b'], 'L0_attn_A_log': _L0_attn_in['A_log'], 'L0_attn_D': _L0_attn_in['D'], 'L0_attn_Bp': _L0_attn_in['Bp'], 'L0_attn_Cp': _L0_attn_in['Cp'], 'L0_attn_Wout': _L0_attn_in['Wout'], 'L0_ffn_g_shared': _L0_ffn_in['g_shared'], 'L0_ffn_W1_s': _L0_ffn_in['W1_s'], 'L0_ffn_b1_s': _L0_ffn_in['b1_s'], 'L0_ffn_W2_s': _L0_ffn_in['W2_s'], 'L0_ffn_b2_s': _L0_ffn_in['b2_s'], 'L0_ffn_g_routed': _L0_ffn_in['g_routed'], 'L0_ffn_W1_r': _L0_ffn_in['W1_r'], 'L0_ffn_b1_r': _L0_ffn_in['b1_r'], 'L0_ffn_W2_r': _L0_ffn_in['W2_r'], 'L0_ffn_b2_r': _L0_ffn_in['b2_r'], 'L0_ffn_centroids': _L0_ffn_in['centroids']}
    _x0 = _d['L0_attn_x']
    _d['L0_attn_x'] = jax.random.normal(jax.random.fold_in(jax.random.key(seed), 1), (8, 512, 128), dtype=_x0.dtype)
    del _x0
    return _d

def reference(L0_attn_x, L0_attn_norm_w, L0_attn_norm_b, L0_attn_Win, L0_attn_conv_w, L0_attn_conv_b, L0_attn_dt_w, L0_attn_dt_b, L0_attn_A_log, L0_attn_D, L0_attn_Bp, L0_attn_Cp, L0_attn_Wout, L0_ffn_g_shared, L0_ffn_W1_s, L0_ffn_b1_s, L0_ffn_W2_s, L0_ffn_b2_s, L0_ffn_g_routed, L0_ffn_W1_r, L0_ffn_b1_r, L0_ffn_W2_r, L0_ffn_b2_r, L0_ffn_centroids):

    def _L0_attn_ref(x, norm_w, norm_b, Win, conv_w, conv_b, dt_w, dt_b, A_log, D, Bp, Cp, Wout):
        import jax, jax.numpy as jnp
        import numpy as np
        from jax import lax
        D_MODEL = 128
        D_STATE = 64
        D_CONV = 4
        EXPAND = 2
        D_INNER = D_MODEL * EXPAND
        BATCH = 2
        T = 128
        EPS = 1e-05
        B_sz, T_len, _ = x.shape
        mu = jnp.mean(x, -1, keepdims=True)
        var = jnp.mean(jnp.square(x - mu), -1, keepdims=True)
        h = (x - mu) * lax.rsqrt(var + EPS) * norm_w + norm_b
        xz = h @ Win
        x_ssm, z = jnp.split(xz, 2, axis=-1)
        xc = jnp.pad(x_ssm, ((0, 0), (D_CONV - 1, 0), (0, 0))).transpose(0, 2, 1)
        xconv = lax.conv_general_dilated(xc, conv_w, (1,), 'VALID', dimension_numbers=('NCH', 'OIH', 'NCH'), feature_group_count=D_INNER)
        x_ssm = jax.nn.silu(xconv.transpose(0, 2, 1) + conv_b)
        dt = jax.nn.softplus(x_ssm @ dt_w + dt_b)
        A = -jnp.exp(A_log)
        Bt = x_ssm @ Bp
        Ct = x_ssm @ Cp

        def step(state, inp):
            x_t, dt_t, B_t, C_t = inp
            dA = jnp.exp(dt_t[:, :, None] * A[None])
            state = state * dA + (dt_t * x_t)[:, :, None] * B_t[:, None, :]
            y_t = jnp.einsum('bds,bs->bd', state, C_t)
            return (state, y_t)
        state0 = jnp.zeros((B_sz, D_INNER, D_STATE), x.dtype)
        xs = (x_ssm.transpose(1, 0, 2), dt.transpose(1, 0, 2), Bt.transpose(1, 0, 2), Ct.transpose(1, 0, 2))
        _, ys = lax.scan(step, state0, xs)
        y = ys.transpose(1, 0, 2)
        y = y + x_ssm * D[None, None, :]
        y = y * jax.nn.silu(z)
        return x + y @ Wout

    def _L0_ffn_ref(u, g_shared, W1_s, b1_s, W2_s, b2_s, g_routed, W1_r, b1_r, W2_r, b2_r, centroids):
        import jax, jax.numpy as jnp
        import numpy as np
        B, T, C = (2, 128, 128)
        H = 512
        E_R, E_S, K = (8, 2, 2)

        def _rmsnorm(x, g):
            eps = jnp.finfo(x.dtype).eps
            return x * jax.lax.rsqrt(jnp.mean(x * x, axis=-1, keepdims=True) + eps) * g

        def _experts_mlp(x, g, W1, b1, W2, b2):
            xn = _rmsnorm(x, g)
            h = jnp.einsum('btc,ech->bteh', xn, W1) + b1
            h = jax.nn.gelu(h, approximate=False)
            return jnp.einsum('bteh,ehc->btec', h, W2) + b2
        h_s = _experts_mlp(u, g_shared, W1_s, b1_s, W2_s, b2_s).sum(axis=-2)
        scores = jax.nn.sigmoid(u @ centroids)
        gpk, i_topk = jax.lax.top_k(scores, K)
        gk = gpk / scores.sum(axis=-1, keepdims=True)
        routed_all = _experts_mlp(u, g_routed, W1_r, b1_r, W2_r, b2_r)
        routed_topk = jnp.take_along_axis(routed_all, i_topk[..., None], axis=2)
        h_r = (gk[..., None] * routed_topk).sum(axis=-2)
        return u + h_s + h_r
    x = L0_attn_x
    xn = _layernorm(x, axis=-1)
    s = _L0_attn_ref(xn, L0_attn_norm_w, L0_attn_norm_b, L0_attn_Win, L0_attn_conv_w, L0_attn_conv_b, L0_attn_dt_w, L0_attn_dt_b, L0_attn_A_log, L0_attn_D, L0_attn_Bp, L0_attn_Cp, L0_attn_Wout)
    g = _silu(_L0_ffn_ref(xn, L0_ffn_g_shared, L0_ffn_W1_s, L0_ffn_b1_s, L0_ffn_W2_s, L0_ffn_b2_s, L0_ffn_g_routed, L0_ffn_W1_r, L0_ffn_b1_r, L0_ffn_W2_r, L0_ffn_b2_r, L0_ffn_centroids))
    x = x + s * g
    return x

_drawn_inputs = setup_inputs


def setup_inputs(seed=0):
    import zlib

    import numpy as np

    out = dict(_drawn_inputs(seed))
    spreads = {'L0_attn_norm_w': (1.0, 0.6),
     'L0_attn_norm_b': (0.0, 0.8),
     'L0_attn_conv_b': (0.0, 0.8),
     'L0_attn_dt_b': (0.0, 0.8),
     'L0_attn_D': (1.0, 0.6),
     'L0_ffn_g_shared': (1.0, 0.6),
     'L0_ffn_g_routed': (1.0, 0.6)}
    factors = {'L0_attn_Win': 8.0,
     'L0_attn_conv_w': 8.0,
     'L0_attn_dt_w': 8.0,
     'L0_attn_A_log': 8.0,
     'L0_attn_Bp': 8.0,
     'L0_attn_Cp': 8.0,
     'L0_attn_Wout': 8.0,
     'L0_ffn_b1_s': 8.0,
     'L0_ffn_b2_s': 5.171,
     'L0_ffn_W1_r': 8.0,
     'L0_ffn_b1_r': 8.0,
     'L0_ffn_W2_r': 8.0,
     'L0_ffn_b2_r': 8.0,
     'L0_ffn_centroids': 8.0}
    for name, (base, spread) in spreads.items():
        noise = np.random.default_rng([zlib.crc32(name.encode()), seed]).standard_normal(out[name].shape)
        drawn = base * np.exp(spread * noise) if base else spread * noise
        out[name] = jnp.asarray(drawn.astype(out[name].dtype))
    for name, factor in factors.items():
        out[name] = (out[name] * factor).astype(out[name].dtype)
    return out
```

```python
from contextlib import ExitStack

import concourse.bass as bass
from concourse import mybir

F32 = mybir.dt.float32
BF16 = mybir.dt.bfloat16
ALU = mybir.AluOpType
ACT = mybir.ActivationFunctionType
X_AXIS = mybir.AxisListType.X
ds = bass.ds

P = 128
F32_EPS = 1.1920928955078125e-07
LN_EPS = 1e-5


def mamba_gated_moe(nc, x, norm_w, norm_b, Win, conv_w, conv_b, dt_w, dt_b, A_log, Dskip, Bp, Cp, Wout,
                    g_shared, W1_s, b1_s, W2_s, b2_s, g_routed, W1_r, b1_r, W2_r, b2_r, centroids, out):
    NB, L, C = x.shape
    T = NB * L
    NT = T // P
    TPB = L // P
    DI, S = A_log.shape
    NH = DI // P
    K = conv_w.shape[2]
    E, _, H = W1_r.shape
    ES = W1_s.shape[0]
    HT = H // P
    SG = S // E
    assert ES * HT == E and S % E == 0 and NH == 2
    SQ = S // 2
    TAPE = 2 * SG
    CG = SG // 2

    ctx = ExitStack()
    with ctx:
        def sb(name, shape, dt=F32):
            return ctx.enter_context(nc.sbuf_tensor(name, shape, dt))

        def sem(name):
            return ctx.enter_context(nc.semaphore(name))

        def dram(name, shape):
            return nc.dram_tensor(name, shape, F32, kind="Internal").ap()

        dt_d = dram("dt_scratch", (NH, P, T))
        u_d = dram("u_scratch", (NH, P, T))
        xs_d = dram("xs_scratch", (NH, P, T))
        sz_d = dram("sz_scratch", (NH, P, T))
        xn_d = dram("xn_scratch", (P, T))
        c_d = dram("c_scratch", (S, T))
        gate_d = dram("gate_scratch", (E, T))
        w1sh_d = dram("w1_shared_tiles", (ES * HT, C, P))
        w2sh_d = dram("w2_shared_tiles", (ES * HT, P, C))

        ident = sb("ident", [P, P])
        x_rs = sb("x_rms_shared", [P, T])
        x_rr = sb("x_rms_routed", [P, T])
        b_parts = sb("b_parts", [3 * SQ, 2, T + L], BF16)
        pick = sb("pick", [3 * SQ, SQ, P], BF16)
        win_sb = sb("win_sb", [P, 2 * DI])
        dtw_sb = sb("dtw_sb", [P, NH, DI])
        bp_sb = sb("bp_sb", [P, NH, S])
        cp_sb = sb("cp_sb", [P, NH, S])
        wout_sb = sb("wout_sb", [P, NH, C])
        cent_sb = sb("cent_sb", [P, E])
        nA = sb("neg_A", [P, NH, S])
        convw_sb = sb("convw_sb", [P, NH, K])
        vecs = sb("vecs", [P, 12])
        NW, NBI, GS, GR = (vecs[:, i:i + 1] for i in range(4))
        CBI = [vecs[:, 4 + h:5 + h] for h in range(NH)]
        DTB = [vecs[:, 6 + h:7 + h] for h in range(NH)]
        DSK = [vecs[:, 8 + h:9 + h] for h in range(NH)]
        diagD = sb("diagD", [P, NH, P])
        b1r_sb = sb("b1r_sb", [P, E * HT])
        b1s_sb = sb("b1s_sb", [P, ES * HT])
        b2r_sb = sb("b2r_sb", [E, C])
        b2s_sb = sb("b2s_sb", [ES, C])
        ones_s = sb("ones_s", [ES, L])
        zrow = sb("zrow", [1, L], BF16)
        tri = sb("tri", [P, E, E])

        TF = T
        arena = sb("arena", [P, ARENA])
        reg = [arena[:, i * TF:(i + 1) * TF] for i in range(6)]
        tok = [r.rearrange("p (j c) -> p j c", c=C) for r in reg]
        X, XN, SQX, HN = tok[0], tok[1], tok[2], tok[3]
        XNT, HTT = reg[0], reg[4]
        cur = [TF]

        def take(size, shape=None, **kw):
            a = arena[:, cur[0]:cur[0] + size]
            cur[0] += size
            return a.rearrange(shape, **kw) if shape else a
        XP = take(NH * (L + K - 1), "p (h t) -> p h t", h=NH)
        CV = take(NH * L, "p (h t) -> p h t", h=NH)
        XS = take(NH * L, "p (h t) -> p h t", h=NH)
        SZ = take(NH * L, "p (h t) -> p h t", h=NH)
        V = take(NH * L, "p (h t) -> p h t", h=NH)
        EX = take(NH * L, "p (h t) -> p h t", h=NH)
        LW = take(NH * L, "p (h t) -> p h t", h=NH)
        WM = take(NH * L, "p (h t) -> p h t", h=NH)
        DT = take(NH * L, "p (h t) -> p h t", h=NH)
        U = take(NH * L, "p (h t) -> p h t", h=NH)
        RB = take(L)[0:S, :]
        BH = take(3 * L // 2).bitcast(BF16).rearrange("p (k t) -> p k t", k=3)[0:S]
        CS = take(L)[0:S, :]
        assert cur[0] <= 4 * TF
        sc = sb("scores", [P, NT, E])
        rank = sb("rank", [P, NT, E])
        st = sb("stats", [P, 8, NT])
        GT = reg[5][0:E, :]

        cur[0] = 0
        dA = take(TAPE * L, "p (n t) -> p n t", t=L)
        CB = take(2 * CG * L, "p (q s t) -> p q s t", q=2, s=CG)
        hs = take(2 * NH * L, "p (n h t) -> p n h t", n=2, h=NH)
        pr = take(2 * NH * L, "p (n h t) -> p n h t", n=2, h=NH)
        dtb = take(2 * NH * L, "p (n h t) -> p n h t", n=2, h=NH)
        ub = take(2 * NH * L, "p (n h t) -> p n h t", n=2, h=NH)
        hid = take((HT + 1) * L, "p (n t) -> p n t", t=L)
        xsb = take(NH * L, "p (h t) -> p h t", h=NH)
        szb = take(NH * L, "p (h t) -> p h t", h=NH)
        xnb = take(L)
        xb = take(L, "p (j c) -> p j c", c=C)
        yg = take(NH * L, "p (h t) -> p h t", h=NH)
        sS = take(L)
        fS = take(L)
        gated = take(L)
        res = take(L, "p (j c) -> p j c", c=C)
        w1b = take((HT + 1) * P, "p (n k) -> p n k", k=P)
        w2b = take((HT + 1) * P, "p (n k) -> p n k", k=P)
        gateb = take(L)
        gtb = take(L)[0:E, :]
        fgate = take(L)
        assert cur[0] <= ARENA, cur[0]

        ps = [ctx.enter_context(nc.psum_tensor(f"ps{i}", [P, L], F32)) for i in range(8)]
        Bbc, dBx, acc, fh, fo, ft = ps[0], ps[1], ps[2:4], ps[4:6], ps[6], ps[7]

        s = {n: sem("s_" + n) for n in (
            "const x w mask neg vch ach xc sq var sd xn hsq hvar hn tr evA evV score sig gate gtr gtc "
            "scr xnout win xpz conv xs dtp bpp cpp vexp ln cc bh dtu dump bmv pad "
            "bbc mul scan da prod ysum c0 c1 dtl fin w1l w2l gl w1u w2u fh gelu fo fg fgu "
            "acc yg wo tot s silu gated trf res store").split()}

        bc3 = lambda a, n: a.unsqueeze(2).broadcast_to((P, NT, n))

        block = ctx.enter_context(nc.Block())

        @block.sync
        def _(sp):
            sp.sem_inc(s["dump"], 16 * N_DUMP)
            sp.sem_inc(s["store"], 16)
            sp.dma_start(X, x.rearrange("b (j p) c -> p (b j) c", p=P)).then_inc(s["x"], 16)
            n = 0
            for dst, src in (
                    (win_sb[:], Win), (dtw_sb[:], dt_w.rearrange("(h p) n -> p h n", p=P)),
                    (bp_sb[:], Bp.rearrange("(h p) n -> p h n", p=P)),
                    (cp_sb[:], Cp.rearrange("(h p) n -> p h n", p=P)),
                    (wout_sb[:], Wout.rearrange("(h p) n -> p h n", p=P)), (cent_sb[:], centroids),
                    (nA[:], A_log.rearrange("(h p) n -> p h n", p=P)),
                    (convw_sb[:], conv_w.rearrange("(h p) o k -> p h (o k)", p=P)),
                    (NW, norm_w.unsqueeze(1)), (NBI, norm_b.unsqueeze(1)),
                    (GS, g_shared.unsqueeze(1)), (GR, g_routed.unsqueeze(1)),
                    (vecs[:, 4:6], conv_b.rearrange("(h p) -> p h", p=P)),
                    (vecs[:, 6:8], dt_b.rearrange("(h p) -> p h", p=P)),
                    (vecs[:, 8:10], Dskip.rearrange("(h p) -> p h", p=P)),
                    (b1r_sb[:], b1_r.rearrange("e (t p) -> p (e t)", p=P)),
                    (b1s_sb[:], b1_s.rearrange("e (t p) -> p (e t)", p=P)),
                    (b2r_sb[:], b2_r), (b2s_sb[:], b2_s)):
                with nc.allow_non_contiguous_dma(reason="small per-channel vectors"):
                    sp.dma_start(dst, src).then_inc(s["w"], 16)
                n += 1
            for e in range(ES):
                sp.dma_start(w1sh_d[e * HT:(e + 1) * HT],
                             W1_s[e].rearrange("c (t h) -> t c h", h=P)).then_inc(s["w"], 16)
                sp.dma_start(w2sh_d[e * HT:(e + 1) * HT],
                             W2_s[e].rearrange("(t h) c -> t h c", h=P)).then_inc(s["w"], 16)
                n += 2
            assert n == N_W
            sp.wait_ge(s["evV"], EVV_XN)
            sp.dma_start(xn_d, XNT).then_inc(s["xnout"], 16)
            sp.wait_ge(s["gtc"], NB)
            sp.dma_start(gate_d, GT).then_inc(s["scr"], 16)
            with sp.Fori(0, NB) as b:
                t0 = sp.snap(b * L)
                sp.wait_ge(s["xs"], b * NH + 2 * NH)
                sp.dma_start(xs_d[:, :, ds(t0, L)].rearrange("h p t -> p h t"), XS).then_inc(s["dump"], 16)
                sp.wait_ge(s["xpz"], b + 2)
                sp.dma_start(sz_d[:, :, ds(t0, L)].rearrange("h p t -> p h t"), SZ).then_inc(s["dump"], 16)
                sp.wait_ge(s["cc"], b + 2)
                sp.dma_start(c_d[:, ds(t0, L)], CS).then_inc(s["dump"], 16)
                sp.wait_ge(s["bh"], b + 2)
                for k in range(3):
                    for q in range(2):
                        sp.dma_start(b_parts[k * SQ:(k + 1) * SQ, q, ds(t0, L)],
                                     BH[q * SQ:(q + 1) * SQ, k, :]).then_inc(s["dump"], 16)
                sp.wait_ge(s["dtu"], b + 2)
                sp.dma_start(dt_d[:, :, ds(t0, L)].rearrange("h p t -> p h t"), DT).then_inc(s["dump"], 16)
                sp.dma_start(u_d[:, :, ds(t0, L)].rearrange("h p t -> p h t"), U).then_inc(s["dump"], 16)

            sp.wait_ge(s["dump"], 16 * N_DUMP * (NB + 1))
            sp.wait_ge(s["xnout"], 16)
            sp.wait_ge(s["scr"], 16)
            sp.wait_ge(s["w"], 16 * N_W)

            for dst, src in ((dtb, dt_d), (ub, u_d)):
                sp.dma_start(dst[:, 0, :, :], src[:, :, 0:L].rearrange("h p t -> p h t")).then_inc(s["dtl"], 16)
            with sp.Fori(0, NB) as b:
                nb = sp.snap(((b + 1) % NB) * L)
                slot = sp.snap(((b + 1) % 2) * (NH * L))
                sp.wait_ge(s["scan"], b * (2 * S) + TAPE)
                sp.wait_ge(s["dtl"], b * 32 + 32)
                for dst, src in ((dtb, dt_d), (ub, u_d)):
                    flat = dst.rearrange("p n h t -> p (n h t)")
                    sp.dma_start(flat[:, ds(slot, NH * L)].rearrange("p (h t) -> p h t", h=NH),
                                 src[:, :, ds(nb, L)].rearrange("h p t -> p h t")).then_inc(s["dtl"], 16)
                with sp.Fori(0, E) as g:
                    for half in range(2):
                        srow = sp.snap(g * SG + half * CG)
                        tb = sp.snap(b * L)
                        sp.wait_ge(s["prod"], (b * S + g * SG) + (half * CG + CG))
                        sp.dma_start(CB[:, half, :, :],
                                     c_d[ds(srow, CG), ds(tb, L)].unsqueeze(0).broadcast_to((P, CG, L))
                                     ).then_inc(s[f"c{half}"], 16)
                        if half == 0:
                            sp.wait_ge(s["w1u"], b * E + g + 1)
                            sp.dma_start(w1b[:, 0:HT, :].rearrange("p n k -> p (n k)"),
                                         W1_r[ds(g, 1)].rearrange("e c h -> (e c) h")).then_inc(s["w1l"], 16)
                            sp.dma_start(w1b[:, HT, :], w1sh_d[ds(g, 1)].rearrange("e c h -> (e c) h")
                                         ).then_inc(s["w1l"], 16)
                        else:
                            sp.wait_ge(s["w2u"], b * E + g + 1)
                            sp.dma_start(w2b[:, 0:HT, :],
                                         W2_r[ds(g, 1)].rearrange("e (t h) c -> (e h) t c", h=P)).then_inc(s["w2l"], 16)
                            sp.dma_start(w2b[:, HT, :], w2sh_d[ds(g, 1)].rearrange("e h c -> (e h) c")
                                         ).then_inc(s["w2l"], 16)
                            sp.wait_ge(s["fg"], b * E + g + 1)
                            sp.dma_start(gateb, gate_d[ds(g, 1), ds(tb, L)].broadcast_to((P, L))
                                         ).then_inc(s["gl"], 16)
                tb = sp.snap(b * L)
                sp.wait_ge(s["res"], b + 1)
                sp.dma_start(xsb, xs_d[:, :, ds(tb, L)].rearrange("h p t -> p h t")).then_inc(s["fin"], 16)
                sp.dma_start(szb, sz_d[:, :, ds(tb, L)].rearrange("h p t -> p h t")).then_inc(s["fin"], 16)
                sp.dma_start(xnb, xn_d[:, ds(tb, L)]).then_inc(s["fin"], 16)
                sp.dma_start(gtb, gate_d[:, ds(tb, L)]).then_inc(s["fin"], 16)
                sp.dma_start(xb, x[ds(b, 1)].rearrange("b (j p) c -> p (b j) c", p=P)).then_inc(s["fin"], 16)
                sp.wait_ge(s["res"], b + 2)
                sp.dma_start(out[ds(b, 1)].rearrange("b (j p) c -> p (b j) c", p=P), res).then_inc(s["store"], 16)
            sp.wait_ge(s["store"], 16 * NB + 16)
            sp.wait_ge(s["dtl"], 32 * (NB + 1))

        @block.gpsimd
        def _(pool):
            m = s["mask"]
            nc.gpsimd.memset(ident[:], 0.0).then_inc(m, 1)
            nc.gpsimd.memset(pick[:], 0.0).then_inc(m, 1)
            nc.gpsimd.memset(tri[:], 1.0).then_inc(m, 1)
            pool.wait_ge(m, 3)
            nc.gpsimd.affine_select(out=ident[:], in_=ident[:], compare_op=ALU.not_equal, fill=1.0, base=0,
                                    pattern=[[-1, P]], channel_multiplier=1).then_inc(m, 1)
            for k in range(3):
                nc.gpsimd.affine_select(out=pick[:], in_=pick[:], compare_op=ALU.not_equal, fill=1.0, base=-k * SQ,
                                        pattern=[[-1, SQ], [0, P]], channel_multiplier=1).then_inc(m, 1)
                pool.wait_ge(m, 5 + k)
            nc.gpsimd.affine_select(out=tri[:], in_=tri[:], compare_op=ALU.is_gt, fill=0.0, base=0,
                                    pattern=[[1, E], [-1, E]], channel_multiplier=0).then_inc(m, 1)
            nc.gpsimd.memset(ones_s[:], 1.0).then_inc(m, 1)
            nc.gpsimd.memset(zrow[:], 0.0).then_inc(m, 1)
            nc.gpsimd.memset(b_parts[:, :, T:T + L], 0.0).then_inc(m, 1)
            assert N_MASK == 11
            pool.drain().then_inc(s["prod"], 2 * CG)
            with pool.Fori(0, NB) as b:
                with pool.Fori(0, E) as g:
                    for i in range(SG):
                        n = b * S + g * SG
                        if i % CG == 0:
                            pool.wait_ge(s[f"c{i // CG}"], (b * E + g + 1) * 16)
                        pool.wait_ge(s["ysum"], n + (i + 1))
                        pool.wait_ge(s["scan"], n * 2 + (TAPE + 2 * i + 2))
                        nc.gpsimd.tensor_tensor(
                            pr[:, i % 2, :, :], hs[:, i % 2, :, :],
                            CB[:, i // CG, i % CG, :].unsqueeze(1).broadcast_to((P, NH, L)),
                            ALU.mult).then_inc(s["prod"], 1)

        @block.scalar
        def _(act):
            chain = [0]

            def link(ins):
                chain[0] += 1
                ins.then_inc(s["ach"], 1)
                act.wait_ge(s["ach"], chain[0])

            act.wait_ge(s["w"], 16 * N_W)
            link(nc.scalar.activation(nA[:], nA[:], ACT.Exp))
            link(nc.scalar.activation(nA[:], nA[:], ACT.Copy, scale=-1.0))
            act.wait_ge(s["xc"], 1)
            nc.scalar.activation(SQX, XN, ACT.Square).then_inc(s["sq"], 1)
            act.wait_ge(s["var"], 1)
            nc.scalar.activation(st[:, 2, :], st[:, 1, :], ACT.Sqrt).then_inc(s["sd"], 1)
            act.wait_ge(s["xn"], 1)
            nc.scalar.activation(SQX, HN, ACT.Square).then_inc(s["sq"], 1)
            act.wait_ge(s["var"], 2)
            nc.scalar.activation(st[:, 6:8, :], st[:, 4:6, :], ACT.Sqrt).then_inc(s["sd"], 1)
            for b in range(NB):
                act.wait_ge(s["tr"], 3 * b + 2)
                nc.scalar.activation(HTT[:, b * L:(b + 1) * L], ps[(3 * b + 1) % 8][:], ACT.Identity,
                                     scale=NW, bias=NBI).then_inc(s["evA"], 1)
                act.wait_ge(s["evV"], 2 * b + 2)
                nc.scalar.activation(x_rs[:, b * L:(b + 1) * L], ps[(3 * b + 2) % 8][:], ACT.Copy,
                                     scale=GS).then_inc(s["evA"], 1)
            act.wait_ge(s["score"], 1)
            nc.scalar.activation(sc[:].rearrange("p j e -> p (j e)"), ps[0][:, 0:NT * E], ACT.Sigmoid).then_inc(s["sig"], 1)
            for b in range(NB):
                act.wait_ge(s["gtr"], b + 1)
                nc.scalar.copy(GT[:, b * L:(b + 1) * L], ps[b][0:E, :]).then_inc(s["gtc"], 1)
            base = chain[0]
            NL = 3
            for name, free in (("xs", NH), ("pad", NH), ("xpz", 1), ("ln", 1), ("cc", 1)):
                act.sem_inc(s[name], free)
            with act.Fori(0, NB) as b:
                def lnk(ins, k):
                    ins.then_inc(s["ach"], 1)
                    act.wait_ge(s["ach"], b * NL + (base + k))
                act.wait_ge(s["win"], b * 4 + 2)
                act.wait_ge(s["conv"], b * NH + NH)
                for h in range(NH):
                    nc.scalar.copy(XP[:, h, K - 1:K - 1 + L], ps[h][:]).then_inc(s["pad"], 1)
                act.wait_ge(s["win"], b * 4 + 4)
                act.wait_ge(s["dump"], b * (16 * N_DUMP) + 16 * N_DUMP)
                nc.scalar.activation(SZ[:, 0, :], ps[2][:], ACT.Silu)
                nc.scalar.activation(SZ[:, 1, :], ps[3][:], ACT.Silu).then_inc(s["xpz"], 1)
                for h in range(NH):
                    act.wait_ge(s["conv"], b * NH + (NH + h + 1))
                    nc.scalar.activation(XS[:, h, :], CV[:, h, :], ACT.Silu, bias=CBI[h]).then_inc(s["xs"], 1)
                act.wait_ge(s["dtp"], b + 1)
                act.wait_ge(s["dtu"], b + 1)
                nc.scalar.activation(V[:, 0, :], ps[4][:], ACT.Identity, bias=DTB[0])
                lnk(nc.scalar.activation(V[:, 1, :], ps[5][:], ACT.Identity, bias=DTB[1]), 1)
                lnk(nc.scalar.activation(EX, V, ACT.Abs), 2)
                nc.scalar.activation(EX, EX, ACT.Exp, scale=-1.0).then_inc(s["vexp"], 1)
                act.wait_ge(s["vexp"], b + 1)
                nc.scalar.activation(LW, EX, ACT.Ln, bias=1.0).then_inc(s["ln"], 1)
                act.wait_ge(s["cpp"], b + 1)
                nc.scalar.copy(CS, ps[7][0:S, :]).then_inc(s["cc"], 1)
                lnk(nc.scalar.copy(vecs[:, 11:12], NW), 3)

            act.sem_inc(s["gelu"], 1)
            act.wait_ge(s["dump"], 16 * N_DUMP * (NB + 1))
            act.wait_ge(s["dtu"], NB + 1)
            with act.Fori(0, NB) as b:
                slot = act.snap((b % 2) * (NH * L))
                act.wait_ge(s["dtl"], b * 32 + 32)
                with act.Fori(0, E) as g:
                    u = b * E + g
                    m0 = (b * E + g) * TAPE
                    dflat = dtb.rearrange("p n h t -> p (n h t)")
                    aflat = nA[:].rearrange("p h s -> p (h s)")
                    for i in range(SG):
                        for h in range(NH):
                            act.wait_ge(s["scan"], m0 + (2 * i + h + 1))
                            act.wait_ge(s["w"], 16 * N_W)
                            nc.scalar.activation(dA[:, 2 * i + h, :], dflat[:, ds(slot + h * L, L)], ACT.Exp,
                                                 scale=aflat[:, ds(g * SG + (h * S + i), 1)]).then_inc(s["da"], 1)
                    act.wait_ge(s["w2u"], u + 1)
                    for t in range(HT + 1):
                        bias = b1r_sb[:, ds(g * HT + t, 1)] if t < HT else b1s_sb[:, ds(g, 1)]
                        act.wait_ge(s["fh"], u * (HT + 1) + (t + 1))
                        act.wait_ge(s["w"], 16 * N_W)
                        nc.scalar.activation(hid[:, t, :], fh[t % 2][:], ACT.Gelu, bias=bias).then_inc(s["gelu"], 1)
                act.wait_ge(s["s"], b * 2 + 4)
                nc.scalar.activation(gated, fS, ACT.Silu).then_inc(s["silu"], 1)

        @block.vector
        def _(dve):
            chain = [0]

            def link(ins):
                chain[0] += 1
                ins.then_inc(s["vch"], 1)
                dve.wait_ge(s["vch"], chain[0])
            V_ = nc.vector
            dve.wait_ge(s["x"], 16)
            link(V_.reduce_sum(st[:, 0, :], X, X_AXIS))
            link(V_.tensor_scalar(st[:, 0, :], st[:, 0, :], 1.0 / C, None, ALU.mult))
            V_.tensor_tensor(XN, X, bc3(st[:, 0, :], C), ALU.subtract).then_inc(s["xc"], 1)
            dve.wait_ge(s["sq"], 1)
            link(V_.reduce_sum(st[:, 1, :], SQX, X_AXIS))
            V_.tensor_scalar(st[:, 1, :], st[:, 1, :], 1.0 / C, LN_EPS, ALU.mult, ALU.add).then_inc(s["var"], 1)
            dve.wait_ge(s["sd"], 1)
            link(V_.reciprocal(st[:, 2, :], st[:, 2, :]))
            link(V_.tensor_tensor(XN, XN, bc3(st[:, 2, :], C), ALU.mult))
            link(V_.reduce_sum(st[:, 3, :], XN, X_AXIS))
            link(V_.tensor_scalar(st[:, 3, :], st[:, 3, :], 1.0 / C, None, ALU.mult))
            V_.tensor_tensor(HN, XN, bc3(st[:, 3, :], C), ALU.subtract).then_inc(s["xn"], 1)
            dve.wait_ge(s["sq"], 2)
            link(V_.reduce_sum(st[:, 4, :], SQX, X_AXIS))
            link(V_.tensor_scalar(st[:, 4, :], st[:, 4, :], 1.0 / C, None, ALU.mult))
            link(V_.tensor_tensor(st[:, 5, :], st[:, 3, :], st[:, 3, :], ALU.mult))
            link(V_.scalar_tensor_tensor(st[:, 5, :], st[:, 5, :], F32_EPS, st[:, 4, :], ALU.add, ALU.add))
            V_.tensor_scalar(st[:, 4, :], st[:, 4, :], LN_EPS, None, ALU.add).then_inc(s["var"], 1)
            dve.wait_ge(s["sd"], 2)
            link(V_.reciprocal(st[:, 6:8, :], st[:, 6:8, :]))
            V_.tensor_tensor(HN, HN, bc3(st[:, 6, :], C), ALU.mult).then_inc(s["hn"], 1)
            V_.tensor_tensor(SQX, XN, bc3(st[:, 7, :], C), ALU.mult).then_inc(s["hn"], 1)
            dve.wait_ge(s["w"], 16 * N_W)
            for b in range(NB):
                dve.wait_ge(s["tr"], 3 * b + 1)
                V_.tensor_copy(XNT[:, b * L:(b + 1) * L], ps[3 * b % 8][:]).then_inc(s["evV"], 1)
                dve.wait_ge(s["tr"], 3 * b + 3)
                V_.tensor_scalar(x_rr[:, b * L:(b + 1) * L], ps[(3 * b + 2) % 8][:], GR, None,
                                 ALU.mult).then_inc(s["evV"], 1)
            dve.wait_ge(s["mask"], N_MASK)
            for h in range(NH):
                V_.tensor_scalar(diagD[:, h, :], ident[:], DSK[h], None, ALU.mult).then_inc(s["evV"], 1)
            dve.wait_ge(s["sig"], 1)
            for h in range(2):
                j = slice(h * NT // 2, (h + 1) * NT // 2)
                hb = (P, NT // 2, E, E)
                oth = sc[:, j, :].unsqueeze(2).broadcast_to(hb)
                own = sc[:, j, :].unsqueeze(3).broadcast_to(hb)
                A4 = reg[5][:, 0:NT // 2 * E * E].rearrange("p (j a b) -> p j a b", a=E, b=E)
                B4 = reg[5][:, NT // 2 * E * E:NT * E * E].rearrange("p (j a b) -> p j a b", a=E, b=E)
                link(V_.tensor_tensor(A4, oth, own, ALU.is_equal))
                link(V_.tensor_tensor(A4, A4, tri[:].unsqueeze(1).broadcast_to(hb), ALU.mult))
                link(V_.tensor_tensor(B4, oth, own, ALU.is_gt))
                link(V_.tensor_tensor(A4, A4, B4, ALU.add))
                link(V_.reduce_sum(rank[:, j, :], A4, X_AXIS))
            link(V_.scalar_tensor_tensor(rank[:].rearrange("p j e -> p (j e)"), rank[:].rearrange("p j e -> p (j e)"),
                                         1.5, sc[:].rearrange("p j e -> p (j e)"), ALU.is_lt, ALU.mult))
            link(V_.reduce_sum(st[:, 0, :], sc[:], X_AXIS))
            link(V_.reciprocal(st[:, 0, :], st[:, 0, :]))
            V_.tensor_tensor(rank[:], rank[:], bc3(st[:, 0, :], E), ALU.mult).then_inc(s["gate"], 1)
            dve.wait_ge(s["tr"], 3 * NB)
            link(V_.memset(XP[:, :, 0:K - 1], 0.0))
            dve.sem_inc(s["conv"], NH)
            dve.sem_inc(s["dtu"], 1)
            dve.sem_inc(s["bh"], 1)
            base, NL = chain[0], NH * (K - 1) + 6
            with dve.Fori(0, NB) as b:
                k = [0]

                def lnk(ins):
                    k[0] += 1
                    ins.then_inc(s["vch"], 1)
                    dve.wait_ge(s["vch"], b * NL + (base + k[0]))
                dve.wait_ge(s["pad"], b * NH + 2 * NH)
                dve.wait_ge(s["xs"], b * NH + NH)
                for h in range(NH):
                    lnk(V_.tensor_scalar(CV[:, h, :], XP[:, h, 0:L], convw_sb[:, h, 0:1], None, ALU.mult))
                    for j in range(1, K):
                        ins = V_.scalar_tensor_tensor(CV[:, h, :], XP[:, h, j:j + L], convw_sb[:, h, j:j + 1],
                                                      CV[:, h, :], ALU.mult, ALU.add)
                        lnk(ins) if j < K - 1 else ins.then_inc(s["conv"], 1)
                dve.wait_ge(s["bpp"], b + 1)
                dve.wait_ge(s["dump"], b * (16 * N_DUMP) + 16 * N_DUMP)
                lnk(V_.tensor_copy(BH[:, 0, :], ps[6][0:S, :]))
                V_.tensor_tensor(RB, ps[6][0:S, :], BH[:, 0, :], ALU.subtract).then_inc(s["bmv"], 1)
                dve.wait_ge(s["bmv"], b * 2 + 1)
                lnk(V_.tensor_copy(BH[:, 1, :], RB))
                V_.tensor_tensor(RB, RB, BH[:, 1, :], ALU.subtract).then_inc(s["bmv"], 1)
                dve.wait_ge(s["bmv"], b * 2 + 2)
                V_.tensor_copy(BH[:, 2, :], RB).then_inc(s["bh"], 1)
                dve.wait_ge(s["vexp"], b + 1)
                lnk(V_.tensor_scalar(WM, EX, 1.0, -1.0, ALU.add, ALU.add))
                lnk(V_.tensor_tensor(WM, EX, WM, ALU.subtract))
                dve.wait_ge(s["ln"], b + 2)
                lnk(V_.tensor_tensor(WM, WM, LW, ALU.add))
                flat = lambda a: a.rearrange("p h t -> p (h t)")
                lnk(V_.scalar_tensor_tensor(flat(DT), flat(V), 0.0, flat(WM), ALU.max, ALU.add))
                V_.tensor_tensor(U, DT, XS, ALU.mult).then_inc(s["dtu"], 1)
                assert k[0] == NL, (k[0], NL)

            dve.wait_ge(s["dump"], 16 * N_DUMP * (NB + 1))
            dve.sem_inc(s["scan"], TAPE)
            dve.sem_inc(s["mul"], NH)
            dve.sem_inc(s["fg"], 1)
            dve.sem_inc(s["res"], 1)
            dve.sem_inc(s["yg"], NH)
            dve.sem_inc(s["s"], 2)
            with dve.Fori(0, NB) as b:
                slot = dve.snap((b % 2) * (NH * L))
                uflat = ub.rearrange("p n h t -> p (n h t)")
                with dve.Fori(0, E) as g:
                    m0 = (b * E + g) * TAPE
                    n0 = (b * E + g) * SG
                    for i in range(SG):
                        for h in range(NH):
                            m = 2 * i + h
                            if m == 0:
                                dve.wait_ge(s["dtl"], b * 32 + 32)
                            if h == 0:
                                dve.wait_ge(s["bbc"], n0 + (i + 1))
                            dve.wait_ge(s["scan"], m0 + (m + TAPE))
                            V_.tensor_tensor(dBx[:], uflat[:, ds(slot + h * L, L)], Bbc[:],
                                             ALU.mult).then_inc(s["mul"], 1)
                            if h == 0:
                                dve.wait_ge(s["prod"], n0 + (i + 1 + 2 * CG - 2))
                            dve.wait_ge(s["da"], m0 + (m + 1))
                            dve.wait_ge(s["mul"], m0 + (m + 1 + NH))
                            V_.tensor_tensor_scan(hs[:, i % 2, h, :], dA[:, m, :], dBx[:], 0.0,
                                                  ALU.mult, ALU.add).then_inc(s["scan"], 1)
                    dve.wait_ge(s["gl"], b * (16 * E) + g * 16 + 16)
                    dve.wait_ge(s["fo"], b * E + g + 1)
                    V_.tensor_tensor(fgate, fo[:], gateb, ALU.mult).then_inc(s["fg"], 1)
                dve.wait_ge(s["fin"], b * (16 * N_FIN) + 16 * N_FIN)
                dve.wait_ge(s["acc"], b + 1)
                for h in range(NH):
                    V_.tensor_tensor(yg[:, h, :], acc[h][:], szb[:, h, :], ALU.mult).then_inc(s["yg"], 1)
                dve.wait_ge(s["wo"], b + 1)
                V_.tensor_tensor(sS, fo[:], xnb, ALU.add).then_inc(s["s"], 1)
                V_.tensor_tensor(fS, ft[:], xnb, ALU.add).then_inc(s["s"], 1)
                dve.wait_ge(s["silu"], b + 1)
                V_.tensor_tensor(gated, gated, sS, ALU.mult).then_inc(s["gated"], 1)
                dve.wait_ge(s["trf"], b + 1)
                dve.wait_ge(s["store"], b * 16 + 16)
                V_.tensor_tensor(res, fh[0][:].rearrange("p (j c) -> p j c", c=C), xb, ALU.add).then_inc(s["res"], 1)

        @block.tensor
        def _(pe):
            mm = nc.tensor.matmul
            pe.wait_ge(s["mask"], N_MASK)
            pe.wait_ge(s["w"], 16 * N_W)
            pe.wait_ge(s["hn"], 2)
            for b in range(NB):
                for kind, src in enumerate((XN, HN, SQX)):
                    k = 3 * b + kind
                    if k >= 8:
                        pb, pk = divmod(k - 8, 3)
                        pe.wait_ge(s["evV"], 2 * pb + (2 if pk == 2 else 1))
                        if pk:
                            pe.wait_ge(s["evA"], 2 * pb + pk)
                    for j in range(TPB):
                        ins = nc.tensor.transpose(ps[k % 8][:, j * P:(j + 1) * P], src[:, b * TPB + j, :], ident[:])
                    ins.then_inc(s["tr"], 1)
            pe.wait_ge(s["evV"], 2 * NB)
            pe.wait_ge(s["evA"], 2 * NB)
            for j in range(NT):
                ins = mm(ps[0][:, j * E:(j + 1) * E], XNT[:, j * P:(j + 1) * P], cent_sb[:], start=True, stop=True)
            ins.then_inc(s["score"], 1)
            pe.wait_ge(s["gate"], 1)
            for j in range(NT):
                ins = nc.tensor.transpose(ps[j // TPB][0:E, (j % TPB) * P:(j % TPB + 1) * P], rank[:, j, :], ident[:])
                if j % TPB == TPB - 1:
                    ins.then_inc(s["gtr"], 1)
            pe.wait_ge(s["gtc"], NB)
            with pe.Fori(0, NB) as b:
                t0 = pe.snap(b * L)
                pe.wait_ge(s["pad"], b * NH + NH)
                pe.wait_ge(s["xpz"], b + 1)
                for j in range(2 * NH):
                    mm(ps[j][:], win_sb[:, j * P:(j + 1) * P], HTT[:, ds(t0, L)], start=True, stop=True
                       ).then_inc(s["win"], 1)
                pe.wait_ge(s["ln"], b + 1)
                pe.wait_ge(s["bh"], b + 1)
                pe.wait_ge(s["cc"], b + 1)
                pe.wait_ge(s["xs"], b * NH + 2 * NH)
                for o in range(NH):
                    for h in range(NH):
                        ins = mm(ps[4 + o][:], dtw_sb[:, h, o * P:(o + 1) * P], XS[:, h, :],
                                 start=(h == 0), stop=(h == NH - 1))
                ins.then_inc(s["dtp"], 1)
                for bank, w, done in ((6, bp_sb, "bpp"), (7, cp_sb, "cpp")):
                    for h in range(NH):
                        ins = mm(ps[bank][0:S, :], w[:, h, :], XS[:, h, :], start=(h == 0), stop=(h == NH - 1))
                    ins.then_inc(s[done], 1)

            pe.wait_ge(s["dump"], 16 * N_DUMP * (NB + 1))
            pe.wait_ge(s["ln"], NB + 1)
            pe.wait_ge(s["cc"], NB + 1)
            bflat = b_parts[:].rearrange("p q t -> p (q t)")
            pflat = pick[:].rearrange("p s m -> p (s m)")
            pe.sem_inc(s["ysum"], 2)
            pe.sem_inc(s["w1u"], 1)
            pe.sem_inc(s["w2u"], 1)
            mm(Bbc[:], pick[:, 0, :], b_parts[:, 0, 0:L], start=True, stop=True).then_inc(s["bbc"], 1)

            with pe.Fori(0, NB) as b:
                t0 = pe.snap(b * L)
                pe.wait_ge(s["yg"], b * NH + NH)
                pe.wait_ge(s["s"], b * 2 + 2)
                pe.wait_ge(s["res"], b + 1)
                for h in range(NH):
                    mm(acc[h][:], zrow[:, 0:P], zrow[:], start=True, stop=False)
                mm(ft[:], zrow[:, 0:P], zrow[:], start=True, stop=False)

                def bcast(n0, i, col, sel):
                    pe.wait_ge(s["mul"], n0 * 2 + (2 * i + NH))
                    mm(Bbc[:], pflat[:, ds(sel, P)], bflat[:, ds(col, L)], start=True, stop=True
                       ).then_inc(s["bbc"], 1)

                def ysum(n0, i):
                    pe.wait_ge(s["prod"], n0 + (i + 1 + 2 * CG))
                    for h in range(NH):
                        ins = mm(acc[h][:], ident[:], pr[:, i % 2, h, :], start=False, stop=False)
                    ins.then_inc(s["ysum"], 1)

                def group(g, first):
                    n0 = (b * E + g) * SG
                    u = b * E + g
                    xcol = t0
                    for i in range(SG):
                        if not (first and i == 0):
                            sidx = g * SG + i
                            col = (sidx // SQ) * (T + L) + t0
                            bcast(n0, i, pe.snap(col), pe.snap((sidx % SQ) * P))
                        if not (first and i < 2):
                            ysum(n0, i - 2)
                        if i in (2, 3):
                            for t in ((0, 1), (2, 3, 4))[i - 2]:
                                if t == 0:
                                    pe.wait_ge(s["w1l"], u * 32 + 32)
                                pe.wait_ge(s["gelu"], u * (HT + 1) + (max(t - 1, 0) + 1))
                                src = x_rr if t < HT else x_rs
                                mm(fh[t % 2][:], w1b[:, t, :], src[:, ds(xcol, L)], start=True, stop=True
                                   ).then_inc(s["fh"], 1)
                        if i in (5, 6):
                            for t in ((0, 1), (2, 3, 4))[i - 5]:
                                if t == 0:
                                    pe.wait_ge(s["w2l"], u * 32 + 32)
                                    pe.wait_ge(s["fg"], u + 1)
                                pe.wait_ge(s["gelu"], u * (HT + 1) + (t + 2))
                                if t < HT:
                                    ins = mm(fo[:], w2b[:, t, :], hid[:, t, :], start=(t == 0), stop=(t == HT - 1))
                                    if t == HT - 1:
                                        ins.then_inc(s["fo"], 1)
                                else:
                                    mm(ft[:], w2b[:, t, :], hid[:, t, :], start=False, stop=False
                                       ).then_inc(s["w2u"], 1)
                        if i == 4:
                            pe.wait_ge(s["fh"], (u + 1) * (HT + 1))
                            pe.sem_inc(s["w1u"], 1)
                    pe.wait_ge(s["fg"], u + 2)
                    mm(ft[:], ident[:], fgate, start=False, stop=False).then_inc(s["fgu"], 1)

                group(0, True)
                with pe.Fori(1, E) as g:
                    group(g, False)
                pe.wait_ge(s["mul"], (b + 1) * (2 * S) + NH)
                mm(Bbc[:], pick[:, 0, :], bflat[:, ds(t0 + L, L)], start=True, stop=True).then_inc(s["bbc"], 1)
                ysum((b + 1) * S, -2)
                ysum((b + 1) * S, -1)
                pe.wait_ge(s["fin"], b * (16 * N_FIN) + 16 * N_FIN)
                for h in range(NH):
                    ins = mm(acc[h][:], diagD[:, h, :], xsb[:, h, :], start=False, stop=True)
                ins.then_inc(s["acc"], 1)
                mm(ft[:], b2r_sb[:], gtb, start=False, stop=False)
                mm(ft[:], b2s_sb[:], ones_s[:], start=False, stop=True).then_inc(s["tot"], 1)
                pe.wait_ge(s["fg"], (b + 1) * E + 1)
                for h in range(NH):
                    pe.wait_ge(s["yg"], b * NH + (NH + h + 1))
                    ins = mm(fo[:], wout_sb[:, h, :], yg[:, h, :], start=(h == 0), stop=(h == NH - 1))
                ins.then_inc(s["wo"], 1)
                pe.wait_ge(s["gated"], b + 1)
                for j in range(TPB):
                    ins = nc.tensor.transpose(fh[0][:, j * P:(j + 1) * P], gated[:, j * P:(j + 1) * P], ident[:])
                ins.then_inc(s["trf"], 1)


N_W = 19 + 4
ARENA = 32000
N_MASK = 11
N_DUMP = 3 + 6 + 2
N_FIN = 5
EVV_XN = 16


_INS = ['L0_attn_x', 'L0_attn_norm_w', 'L0_attn_norm_b', 'L0_attn_Win', 'L0_attn_conv_w', 'L0_attn_conv_b',
        'L0_attn_dt_w', 'L0_attn_dt_b', 'L0_attn_A_log', 'L0_attn_D', 'L0_attn_Bp', 'L0_attn_Cp', 'L0_attn_Wout',
        'L0_ffn_g_shared', 'L0_ffn_W1_s', 'L0_ffn_b1_s', 'L0_ffn_W2_s', 'L0_ffn_b2_s', 'L0_ffn_g_routed',
        'L0_ffn_W1_r', 'L0_ffn_b1_r', 'L0_ffn_W2_r', 'L0_ffn_b2_r', 'L0_ffn_centroids']


def kernel(**inputs):
    import numpy as _np
    import concourse.bacc as _bacc
    from concourse import mybir as _mybir
    from concourse.bass_utils import run_bass_kernel_spmd as _run

    nc = _bacc.Bacc("TRN2", target_bir_lowering=False, num_devices=1)
    arrays, args = {}, []
    for name in _INS:
        a = _np.ascontiguousarray(inputs[name])
        arrays[f"in_{name}_dram"] = a
        args.append(nc.dram_tensor(f"in_{name}_dram", a.shape, _mybir.dt.from_np(a.dtype), kind="ExternalInput").ap())
    shape = inputs['L0_attn_x'].shape
    args.append(nc.dram_tensor("out_0_dram", shape, _mybir.dt.float32, kind="ExternalOutput").ap())
    mamba_gated_moe(nc, *args)
    r = _run(nc, [arrays], core_ids=[0])
    return r.results[0]["out_0_dram"]
```

```python
from contextlib import ExitStack

import concourse.bass as bass
from concourse import mybir

F32 = mybir.dt.float32
BF16 = mybir.dt.bfloat16
ALU = mybir.AluOpType
ACT = mybir.ActivationFunctionType
X_AXIS = mybir.AxisListType.X
ds = bass.ds

P = 128
F32_EPS = 1.1920928955078125e-07
LN_EPS = 1e-5


def mamba_gated_moe(nc, x, norm_w, norm_b, Win, conv_w, conv_b, dt_w, dt_b, A_log, Dskip, Bp, Cp, Wout,
                    g_shared, W1_s, b1_s, W2_s, b2_s, g_routed, W1_r, b1_r, W2_r, b2_r, centroids, out):
    NB, L, C = x.shape
    T = NB * L
    NT = T // P
    TPB = L // P
    DI, S = A_log.shape
    NH = DI // P
    K = conv_w.shape[2]
    E, _, H = W1_r.shape
    ES = W1_s.shape[0]
    HT = H // P
    SG = S // E
    assert ES * HT == E and S % E == 0 and NH == 2
    SQ = S // 2
    TAPE = 2 * SG
    HP = P // 2
    CG = SG // 2

    ctx = ExitStack()
    with ctx:
        def sb(name, shape, dt=F32):
            return ctx.enter_context(nc.sbuf_tensor(name, shape, dt))

        def sem(name):
            return ctx.enter_context(nc.semaphore(name))

        def dram(name, shape):
            return nc.dram_tensor(name, shape, F32, kind="Internal").ap()

        dt_d = dram("dt_scratch", (NH, P, T))
        u_d = dram("u_scratch", (NH, P, T))
        xs_d = dram("xs_scratch", (NH, P, T))
        sz_d = dram("sz_scratch", (NH, P, T))
        xn_d = dram("xn_scratch", (P, T))
        c_d = dram("c_scratch", (S, T))
        gate_d = dram("gate_scratch", (E, T))
        w1sh_d = dram("w1_shared_tiles", (ES * HT, C, P))
        w2sh_d = dram("w2_shared_tiles", (ES * HT, P, C))

        ident = sb("ident", [P, P])
        x_rs = sb("x_rms_shared", [P, T])
        x_rr = sb("x_rms_routed", [P, T])
        b_parts = sb("b_parts", [3 * SQ, 2, T], BF16)
        pick = sb("pick", [3 * SQ, SQ, P], BF16)
        win_sb = sb("win_sb", [P, 2 * DI])
        dtw_sb = sb("dtw_sb", [P, NH, DI])
        bp_sb = sb("bp_sb", [P, NH, S])
        cp_sb = sb("cp_sb", [P, NH, S])
        wout_sb = sb("wout_sb", [P, NH, C])
        cent_sb = sb("cent_sb", [P, E])
        nA = sb("neg_A", [P, NH, S])
        convw_sb = sb("convw_sb", [P, NH, K])
        vecs = sb("vecs", [P, 12])
        NW, NBI, GS, GR = (vecs[:, i:i + 1] for i in range(4))
        CBI = [vecs[:, 4 + h:5 + h] for h in range(NH)]
        DTB = [vecs[:, 6 + h:7 + h] for h in range(NH)]
        DSK = [vecs[:, 8 + h:9 + h] for h in range(NH)]
        diagD = sb("diagD", [P, NH, P])
        b1r_sb = sb("b1r_sb", [P, E * HT])
        b1s_sb = sb("b1s_sb", [P, ES * HT])
        b2r_sb = sb("b2r_sb", [E, C])
        b2s_sb = sb("b2s_sb", [ES, C])
        ones_s = sb("ones_s", [ES, L])
        zrow = sb("zrow", [1, L], BF16)
        tri = sb("tri", [P, E, E])

        TF = T
        arena = sb("arena", [P, ARENA])
        reg = [arena[:, i * TF:(i + 1) * TF] for i in range(6)]
        tok = [r.rearrange("p (j c) -> p j c", c=C) for r in reg]
        X, XN, SQX, HN = tok[0], tok[1], tok[2], tok[3]
        XNT, HTT = reg[0], reg[4]
        cur = [TF]

        def take(size, shape=None, **kw):
            a = arena[:, cur[0]:cur[0] + size]
            cur[0] += size
            return a.rearrange(shape, **kw) if shape else a
        XP = take(NH * (L + K - 1), "p (h t) -> p h t", h=NH)
        CV = take(NH * L, "p (h t) -> p h t", h=NH)
        XS = take(NH * L, "p (h t) -> p h t", h=NH)
        SZ = take(NH * L, "p (h t) -> p h t", h=NH)
        V = take(NH * L, "p (h t) -> p h t", h=NH)
        EX = take(NH * L, "p (h t) -> p h t", h=NH)
        LW = take(NH * L, "p (h t) -> p h t", h=NH)
        WM = take(NH * L, "p (h t) -> p h t", h=NH)
        DT = take(NH * L, "p (h t) -> p h t", h=NH)
        U = take(NH * L, "p (h t) -> p h t", h=NH)
        RB = take(L)[0:S, :]
        BH = take(3 * L // 2).bitcast(BF16).rearrange("p (k t) -> p k t", k=3)[0:S]
        CS = take(L)[0:S, :]
        assert cur[0] <= 4 * TF
        sc = sb("scores", [P, NT, E])
        rank = sb("rank", [P, NT, E])
        st = sb("stats", [P, 8, NT])
        GT = reg[5][0:E, :]

        cur[0] = 0
        dA = take(TAPE * L, "p (n t) -> p n t", t=L)
        CB = take(2 * CG * L, "p (q s t) -> p q s t", q=2, s=CG)
        hs = take(2 * NH * L, "p (n h t) -> p n h t", n=2, h=NH)
        pr = take(2 * NH * L, "p (n h t) -> p n h t", n=2, h=NH)
        dtb = take(2 * NH * L, "p (n h t) -> p n h t", n=2, h=NH)
        ub = take(2 * NH * L, "p (n h t) -> p n h t", n=2, h=NH)
        hid = take((HT + 1) * L, "p (n t) -> p n t", t=L)
        xsb = take(NH * L, "p (h t) -> p h t", h=NH)
        szb = take(NH * L, "p (h t) -> p h t", h=NH)
        xnb = take(L)
        xb = take(L, "p (j c) -> p j c", c=C)
        yg = take(NH * L, "p (h t) -> p h t", h=NH)
        sS = take(L)
        fS = take(L)
        gated = take(L)
        res = take(L, "p (j c) -> p j c", c=C)
        w1b = take((HT + 1) * P, "p (n k) -> p n k", k=P)
        w2b = take((HT + 1) * P, "p (n k) -> p n k", k=P)
        gateb = take(L)
        gtb = take(L)[0:E, :]
        fgate = take(L)
        fsum = take(L)
        assert cur[0] <= ARENA, cur[0]

        ps = [ctx.enter_context(nc.psum_tensor(f"ps{i}", [P, L], F32)) for i in range(8)]
        Bbc, dBx, acc, fh, fo, ft = ps[0], ps[1:3], ps[3:5], ps[5:7], ps[6], ps[7]

        s = {n: sem("s_" + n) for n in (
            "const x w mask neg vch ach xc sq var sd xn hsq hvar hn tr evA evV score sig gate gtr gtc "
            "scr xnout win xpz conv xs dtp bpp cpp vexp ln cc bh dtu dump bmv pad "
            "bbc mul scan da prod ysum c0 c1 dtl fin w1l w2l gl w1u w2u fh gelu fo fg fgu "
            "held taken xl acc yg wo tot fs ss silu gated trf res store").split()}

        bc3 = lambda a, n: a.unsqueeze(2).broadcast_to((P, NT, n))

        block = ctx.enter_context(nc.Block())

        @block.sync
        def _(sp):
            sp.sem_inc(s["dump"], 16 * N_DUMP)
            sp.sem_inc(s["store"], 16)
            sp.dma_start(X, x.rearrange("b (j p) c -> p (b j) c", p=P)).then_inc(s["x"], 16)
            n = 0
            for dst, src in (
                    (win_sb[:], Win), (dtw_sb[:], dt_w.rearrange("(h p) n -> p h n", p=P)),
                    (bp_sb[:], Bp.rearrange("(h p) n -> p h n", p=P)),
                    (cp_sb[:], Cp.rearrange("(h p) n -> p h n", p=P)),
                    *((wout_sb[HP * h:HP * h + HP, :, :], Wout[P * h:P * h + P].rearrange("(r q) n -> q r n", q=HP))
                      for h in range(NH)), (cent_sb[:], centroids),
                    (nA[:], A_log.rearrange("(h p) n -> p h n", p=P)),
                    (convw_sb[:], conv_w.rearrange("(h p) o k -> p h (o k)", p=P)),
                    (NW, norm_w.unsqueeze(1)), (NBI, norm_b.unsqueeze(1)),
                    (GS, g_shared.unsqueeze(1)), (GR, g_routed.unsqueeze(1)),
                    (vecs[:, 4:6], conv_b.rearrange("(h p) -> p h", p=P)),
                    (vecs[:, 6:8], dt_b.rearrange("(h p) -> p h", p=P)),
                    *((vecs[HP * h:HP * h + HP, 8:10], Dskip[P * h:P * h + P].rearrange("(r q) -> q r", q=HP))
                      for h in range(NH)),
                    (b1r_sb[:], b1_r.rearrange("e (t p) -> p (e t)", p=P)),
                    (b1s_sb[:], b1_s.rearrange("e (t p) -> p (e t)", p=P)),
                    (b2r_sb[:], b2_r), (b2s_sb[:], b2_s)):
                with nc.allow_non_contiguous_dma(reason="small per-channel vectors"):
                    sp.dma_start(dst, src).then_inc(s["w"], 16)
                n += 1
            for e in range(ES):
                sp.dma_start(w1sh_d[e * HT:(e + 1) * HT],
                             W1_s[e].rearrange("c (t h) -> t c h", h=P)).then_inc(s["w"], 16)
                sp.dma_start(w2sh_d[e * HT:(e + 1) * HT],
                             W2_s[e].rearrange("(t h) c -> t h c", h=P)).then_inc(s["w"], 16)
                n += 2
            assert n == N_W
            sp.wait_ge(s["evV"], EVV_XN)
            sp.dma_start(xn_d, XNT).then_inc(s["xnout"], 16)
            sp.wait_ge(s["gtc"], NB)
            sp.dma_start(gate_d, GT).then_inc(s["scr"], 16)
            with sp.Fori(0, NB) as b:
                t0 = sp.snap(b * L)
                sp.wait_ge(s["xs"], b * NH + 2 * NH)
                sp.dma_start(xs_d[:, :, ds(t0, L)].rearrange("h p t -> p h t"), XS).then_inc(s["dump"], 16)
                sp.wait_ge(s["xpz"], b + 2)
                sp.dma_start(sz_d[:, :, ds(t0, L)].rearrange("h p t -> p h t"), SZ).then_inc(s["dump"], 16)
                sp.wait_ge(s["cc"], b + 2)
                sp.dma_start(c_d[:, ds(t0, L)], CS).then_inc(s["dump"], 16)
                sp.wait_ge(s["bh"], b + 2)
                for k in range(3):
                    for q in range(2):
                        sp.dma_start(b_parts[k * SQ:(k + 1) * SQ, q, ds(t0, L)],
                                     BH[q * SQ:(q + 1) * SQ, k, :]).then_inc(s["dump"], 16)
                sp.wait_ge(s["dtu"], b + 2)
                sp.dma_start(dt_d[:, :, ds(t0, L)].rearrange("h p t -> p h t"), DT).then_inc(s["dump"], 16)
                sp.dma_start(u_d[:, :, ds(t0, L)].rearrange("h p t -> p h t"), U).then_inc(s["dump"], 16)

            sp.wait_ge(s["dump"], 16 * N_DUMP * (NB + 1))
            sp.wait_ge(s["xnout"], 16)
            sp.wait_ge(s["scr"], 16)
            sp.wait_ge(s["w"], 16 * N_W)

            for dst, src in ((dtb, dt_d), (ub, u_d)):
                sp.dma_start(dst[:, 0, :, :], src[:, :, 0:L].rearrange("h p t -> p h t")).then_inc(s["dtl"], 16)
            snap = lambda v: v if isinstance(v, int) else sp.snap(v)

            def load_group(b, g):
                for half in range(2):
                    srow = snap(g * SG + half * CG)
                    tb = snap(b * L)
                    sp.wait_ge(s["prod"], (b * S + g * SG) + (half * CG + CG))
                    sp.dma_start(CB[:, half, :, :],
                                 c_d[ds(srow, CG), ds(tb, L)].unsqueeze(0).broadcast_to((P, CG, L))
                                 ).then_inc(s[f"c{half}"], 16)
                    if half == 0:
                        sp.wait_ge(s["w1u"], b * E + g + 1)
                        sp.dma_start(w1b[:, 0:HT, :].rearrange("p n k -> p (n k)"),
                                     W1_r[ds(g, 1)].rearrange("e c h -> (e c) h")).then_inc(s["w1l"], 16)
                        sp.dma_start(w1b[:, HT, :], w1sh_d[ds(g, 1)].rearrange("e c h -> (e c) h")
                                     ).then_inc(s["w1l"], 16)
                    else:
                        sp.wait_ge(s["w2u"], b * E + g + 1)
                        sp.dma_start(w2b[:, 0:HT, :],
                                     W2_r[ds(g, 1)].rearrange("e (t h) c -> (e h) t c", h=P)).then_inc(s["w2l"], 16)
                        sp.dma_start(w2b[:, HT, :], w2sh_d[ds(g, 1)].rearrange("e h c -> (e h) c")
                                     ).then_inc(s["w2l"], 16)
                        sp.wait_ge(s["fg"], b * E + g + 1)
                        sp.dma_start(gateb, gate_d[ds(g, 1), ds(tb, L)].broadcast_to((P, L))
                                     ).then_inc(s["gl"], 16)

            def store_result(b):
                row = snap(b + 0)
                sp.wait_ge(s["res"], b + 2)
                sp.dma_start(out[ds(row, 1)].rearrange("b (j p) c -> p (b j) c", p=P), res
                             ).then_inc(s["store"], 16)

            def load_block(b, first):
                load_group(b, 0)
                nb = snap(((b + 1) % NB) * L)
                slot = snap(((b + 1) % 2) * (NH * L))
                sp.wait_ge(s["scan"], b * (2 * S) + TAPE)
                sp.wait_ge(s["dtl"], b * 32 + 32)
                for dst, src in ((dtb, dt_d), (ub, u_d)):
                    flat = dst.rearrange("p n h t -> p (n h t)")
                    sp.dma_start(flat[:, ds(slot, NH * L)].rearrange("p (h t) -> p h t", h=NH),
                                 src[:, :, ds(nb, L)].rearrange("h p t -> p h t")).then_inc(s["dtl"], 16)
                tb = snap(b * L)
                if not first:
                    sp.wait_ge(s["ss"], b + 0)
                sp.dma_start(xnb, xn_d[:, ds(tb, L)]).then_inc(s["xl"], 16)
                if not first:
                    store_result(b - 1)
                with sp.Fori(1, E) as g:
                    load_group(b, g)
                row = snap(b + 0)
                sp.wait_ge(s["res"], b + 1)
                for dst, src in ((xsb, xs_d), (szb, sz_d)):
                    for h in range(NH):
                        sp.dma_start(dst[HP * h:HP * h + HP, :, :],
                                     src[h, :, ds(tb, L)].rearrange("(r q) t -> q r t", q=HP)).then_inc(s["fin"], 16)
                sp.dma_start(gtb, gate_d[:, ds(tb, L)]).then_inc(s["fin"], 16)
                sp.dma_start(xb, x[ds(row, 1)].rearrange("b (j p) c -> p (b j) c", p=P)).then_inc(s["fin"], 16)

            load_block(0, True)
            with sp.Fori(1, NB) as b:
                load_block(b, False)
            store_result(NB - 1)
            sp.wait_ge(s["store"], 16 * NB + 16)
            sp.wait_ge(s["dtl"], 32 * (NB + 1))

        @block.gpsimd
        def _(pool):
            m = s["mask"]
            nc.gpsimd.memset(ident[:], 0.0).then_inc(m, 1)
            nc.gpsimd.memset(pick[:], 0.0).then_inc(m, 1)
            nc.gpsimd.memset(tri[:], 1.0).then_inc(m, 1)
            pool.wait_ge(m, 3)
            nc.gpsimd.affine_select(out=ident[:], in_=ident[:], compare_op=ALU.not_equal, fill=1.0, base=0,
                                    pattern=[[-1, P]], channel_multiplier=1).then_inc(m, 1)
            for k in range(3):
                nc.gpsimd.affine_select(out=pick[:], in_=pick[:], compare_op=ALU.not_equal, fill=1.0, base=-k * SQ,
                                        pattern=[[-1, SQ], [0, P]], channel_multiplier=1).then_inc(m, 1)
                pool.wait_ge(m, 5 + k)
            nc.gpsimd.affine_select(out=tri[:], in_=tri[:], compare_op=ALU.is_gt, fill=0.0, base=0,
                                    pattern=[[1, E], [-1, E]], channel_multiplier=0).then_inc(m, 1)
            nc.gpsimd.memset(ones_s[:], 1.0).then_inc(m, 1)
            nc.gpsimd.memset(zrow[:], 0.0).then_inc(m, 1)
            pool.drain().then_inc(s["prod"], 2 * CG)
            pool.sem_inc(s["fgu"], 1)

            def group(b, g, head=False):
                for i in range(SG):
                    n = b * S + g * SG
                    if i % CG == 0:
                        pool.wait_ge(s[f"c{i // CG}"], (b * E + g + 1) * 16)
                    if i == SG - 1:
                        pool.wait_ge(s["fg"], b * E + g + 2)
                        if head:
                            pool.wait_ge(s["fs"], b + 1)
                            pool.wait_ge(s["xl"], b * 16 + 16)
                            nc.gpsimd.tensor_tensor(fsum, xnb, fgate, ALU.add).then_inc(s["fgu"], 1)
                        else:
                            pool.wait_ge(s["fgu"], b * E + g + 1)
                            nc.gpsimd.tensor_tensor(fsum, fsum, fgate, ALU.add).then_inc(s["fgu"], 1)
                    pool.wait_ge(s["ysum"], n + (i + 1))
                    pool.wait_ge(s["scan"], n * 2 + (TAPE + 2 * i + 2))
                    nc.gpsimd.tensor_tensor(
                        pr[:, i % 2, :, :], hs[:, i % 2, :, :],
                        CB[:, i // CG, i % CG, :].unsqueeze(1).broadcast_to((P, NH, L)),
                        ALU.mult).then_inc(s["prod"], 1)

            with pool.Fori(0, NB) as b:
                group(b, 0, head=True)
                with pool.Fori(1, E) as g:
                    group(b, g)

        @block.scalar
        def _(act):
            chain = [0]

            def link(ins):
                chain[0] += 1
                ins.then_inc(s["ach"], 1)
                act.wait_ge(s["ach"], chain[0])

            act.wait_ge(s["w"], 16 * N_W)
            link(nc.scalar.activation(nA[:], nA[:], ACT.Exp))
            link(nc.scalar.activation(nA[:], nA[:], ACT.Copy, scale=-1.0))
            act.wait_ge(s["xc"], 1)
            nc.scalar.activation(SQX, XN, ACT.Square).then_inc(s["sq"], 1)
            act.wait_ge(s["var"], 1)
            nc.scalar.activation(st[:, 2, :], st[:, 1, :], ACT.Sqrt).then_inc(s["sd"], 1)
            act.wait_ge(s["xn"], 1)
            nc.scalar.activation(SQX, HN, ACT.Square).then_inc(s["sq"], 1)
            act.wait_ge(s["var"], 2)
            nc.scalar.activation(st[:, 6:8, :], st[:, 4:6, :], ACT.Sqrt).then_inc(s["sd"], 1)
            for b in range(NB):
                act.wait_ge(s["tr"], 3 * b + 2)
                nc.scalar.activation(HTT[:, b * L:(b + 1) * L], ps[(3 * b + 1) % 8][:], ACT.Identity,
                                     scale=NW, bias=NBI).then_inc(s["evA"], 1)
                act.wait_ge(s["evV"], 2 * b + 2)
                nc.scalar.activation(x_rs[:, b * L:(b + 1) * L], ps[(3 * b + 2) % 8][:], ACT.Copy,
                                     scale=GS).then_inc(s["evA"], 1)
            act.wait_ge(s["score"], 1)
            nc.scalar.activation(sc[:].rearrange("p j e -> p (j e)"), ps[0][:, 0:NT * E], ACT.Sigmoid).then_inc(s["sig"], 1)
            for b in range(NB):
                act.wait_ge(s["gtr"], b + 1)
                nc.scalar.copy(GT[:, b * L:(b + 1) * L], ps[b][0:E, :]).then_inc(s["gtc"], 1)
            base = chain[0]
            NL = 3
            for name, free in (("xs", NH), ("pad", NH), ("xpz", 1), ("ln", 1), ("cc", 1)):
                act.sem_inc(s[name], free)
            with act.Fori(0, NB) as b:
                def lnk(ins, k):
                    ins.then_inc(s["ach"], 1)
                    act.wait_ge(s["ach"], b * NL + (base + k))
                act.wait_ge(s["win"], b * 4 + 2)
                act.wait_ge(s["conv"], b * NH + NH)
                for h in range(NH):
                    nc.scalar.copy(XP[:, h, K - 1:K - 1 + L], ps[h][:]).then_inc(s["pad"], 1)
                act.wait_ge(s["win"], b * 4 + 4)
                act.wait_ge(s["dump"], b * (16 * N_DUMP) + 16 * N_DUMP)
                nc.scalar.activation(SZ[:, 0, :], ps[2][:], ACT.Silu)
                nc.scalar.activation(SZ[:, 1, :], ps[3][:], ACT.Silu).then_inc(s["xpz"], 1)
                for h in range(NH):
                    act.wait_ge(s["conv"], b * NH + (NH + h + 1))
                    nc.scalar.activation(XS[:, h, :], CV[:, h, :], ACT.Silu, bias=CBI[h]).then_inc(s["xs"], 1)
                act.wait_ge(s["dtp"], b + 1)
                act.wait_ge(s["dtu"], b + 1)
                nc.scalar.activation(V[:, 0, :], ps[4][:], ACT.Identity, bias=DTB[0])
                lnk(nc.scalar.activation(V[:, 1, :], ps[5][:], ACT.Identity, bias=DTB[1]), 1)
                lnk(nc.scalar.activation(EX, V, ACT.Abs), 2)
                nc.scalar.activation(EX, EX, ACT.Exp, scale=-1.0).then_inc(s["vexp"], 1)
                act.wait_ge(s["vexp"], b + 1)
                nc.scalar.activation(LW, EX, ACT.Ln, bias=1.0).then_inc(s["ln"], 1)
                act.wait_ge(s["cpp"], b + 1)
                nc.scalar.copy(CS, ps[7][0:S, :]).then_inc(s["cc"], 1)
                lnk(nc.scalar.copy(vecs[:, 11:12], NW), 3)

            act.sem_inc(s["gelu"], 1)
            act.wait_ge(s["dump"], 16 * N_DUMP * (NB + 1))
            act.wait_ge(s["dtu"], NB + 1)
            dflat = dtb.rearrange("p n h t -> p (n h t)")
            aflat = nA[:].rearrange("p h s -> p (h s)")

            snap = lambda v: v if isinstance(v, int) else act.snap(v)

            def group(b, g, slot, last=None):
                u = b * E + g
                m0 = (b * E + g) * TAPE
                for i in range(SG):
                    for h in range(NH):
                        act.wait_ge(s["scan"], m0 + (2 * i + h + 1))
                        act.sem_inc(s["held"], 1)
                        col = snap(g * SG + (h * S + i))
                        nc.scalar.activation(dA[:, 2 * i + h, :], dflat[:, ds(slot + h * L, L)], ACT.Exp,
                                             scale=aflat[:, ds(col, 1)]).then_inc(s["da"], 1)
                act.wait_ge(s["w2u"], u + 1)
                for t in range(HT + 1):
                    bias = b1r_sb[:, ds(g * HT + t, 1)] if t < HT else b1s_sb[:, ds(g, 1)]
                    act.wait_ge(s["fh"], u * (HT + 1) + (t + 1))
                    act.wait_ge(s["w"], 16 * N_W)
                    nc.scalar.activation(hid[:, t, :], fh[t % 2][:], ACT.Gelu, bias=bias).then_inc(s["gelu"], 1)
                if last is not None:
                    silu_of(last)

            def silu_of(b):
                act.wait_ge(s["fs"], b + 2)
                nc.scalar.activation(gated, fS, ACT.Silu).then_inc(s["silu"], 1)

            def run(b, last):
                slot = b if isinstance(b, int) else act.snap((b % 2) * (NH * L))
                act.wait_ge(s["dtl"], b * 32 + 32)
                group(b, 0, slot, last)
                with act.Fori(1, E) as g:
                    group(b, g, slot)
            run(0, None)
            with act.Fori(1, NB) as b:
                run(b, b - 1)
            silu_of(NB - 1)

        @block.vector
        def _(dve):
            chain = [0]

            def link(ins):
                chain[0] += 1
                ins.then_inc(s["vch"], 1)
                dve.wait_ge(s["vch"], chain[0])
            V_ = nc.vector
            dve.wait_ge(s["x"], 16)
            link(V_.reduce_sum(st[:, 0, :], X, X_AXIS))
            link(V_.tensor_scalar(st[:, 0, :], st[:, 0, :], 1.0 / C, None, ALU.mult))
            V_.tensor_tensor(XN, X, bc3(st[:, 0, :], C), ALU.subtract).then_inc(s["xc"], 1)
            dve.wait_ge(s["sq"], 1)
            link(V_.reduce_sum(st[:, 1, :], SQX, X_AXIS))
            V_.tensor_scalar(st[:, 1, :], st[:, 1, :], 1.0 / C, LN_EPS, ALU.mult, ALU.add).then_inc(s["var"], 1)
            dve.wait_ge(s["sd"], 1)
            link(V_.reciprocal(st[:, 2, :], st[:, 2, :]))
            link(V_.tensor_tensor(XN, XN, bc3(st[:, 2, :], C), ALU.mult))
            link(V_.reduce_sum(st[:, 3, :], XN, X_AXIS))
            link(V_.tensor_scalar(st[:, 3, :], st[:, 3, :], 1.0 / C, None, ALU.mult))
            V_.tensor_tensor(HN, XN, bc3(st[:, 3, :], C), ALU.subtract).then_inc(s["xn"], 1)
            dve.wait_ge(s["sq"], 2)
            link(V_.reduce_sum(st[:, 4, :], SQX, X_AXIS))
            link(V_.tensor_scalar(st[:, 4, :], st[:, 4, :], 1.0 / C, None, ALU.mult))
            link(V_.tensor_tensor(st[:, 5, :], st[:, 3, :], st[:, 3, :], ALU.mult))
            link(V_.scalar_tensor_tensor(st[:, 5, :], st[:, 5, :], F32_EPS, st[:, 4, :], ALU.add, ALU.add))
            V_.tensor_scalar(st[:, 4, :], st[:, 4, :], LN_EPS, None, ALU.add).then_inc(s["var"], 1)
            dve.wait_ge(s["sd"], 2)
            link(V_.reciprocal(st[:, 6:8, :], st[:, 6:8, :]))
            V_.tensor_tensor(HN, HN, bc3(st[:, 6, :], C), ALU.mult).then_inc(s["hn"], 1)
            V_.tensor_tensor(SQX, XN, bc3(st[:, 7, :], C), ALU.mult).then_inc(s["hn"], 1)
            dve.wait_ge(s["w"], 16 * N_W)
            for b in range(NB):
                dve.wait_ge(s["tr"], 3 * b + 1)
                V_.tensor_copy(XNT[:, b * L:(b + 1) * L], ps[3 * b % 8][:]).then_inc(s["evV"], 1)
                dve.wait_ge(s["tr"], 3 * b + 3)
                V_.tensor_scalar(x_rr[:, b * L:(b + 1) * L], ps[(3 * b + 2) % 8][:], GR, None,
                                 ALU.mult).then_inc(s["evV"], 1)
            dve.wait_ge(s["mask"], N_MASK)
            for h in range(NH):
                V_.tensor_scalar(diagD[:, h, :], ident[:], DSK[h], None, ALU.mult).then_inc(s["evV"], 1)
            dve.wait_ge(s["sig"], 1)
            for h in range(2):
                j = slice(h * NT // 2, (h + 1) * NT // 2)
                hb = (P, NT // 2, E, E)
                oth = sc[:, j, :].unsqueeze(2).broadcast_to(hb)
                own = sc[:, j, :].unsqueeze(3).broadcast_to(hb)
                A4 = reg[5][:, 0:NT // 2 * E * E].rearrange("p (j a b) -> p j a b", a=E, b=E)
                B4 = reg[5][:, NT // 2 * E * E:NT * E * E].rearrange("p (j a b) -> p j a b", a=E, b=E)
                link(V_.tensor_tensor(A4, oth, own, ALU.is_equal))
                link(V_.tensor_tensor(A4, A4, tri[:].unsqueeze(1).broadcast_to(hb), ALU.mult))
                link(V_.tensor_tensor(B4, oth, own, ALU.is_gt))
                link(V_.tensor_tensor(A4, A4, B4, ALU.add))
                link(V_.reduce_sum(rank[:, j, :], A4, X_AXIS))
            link(V_.scalar_tensor_tensor(rank[:].rearrange("p j e -> p (j e)"), rank[:].rearrange("p j e -> p (j e)"),
                                         1.5, sc[:].rearrange("p j e -> p (j e)"), ALU.is_lt, ALU.mult))
            link(V_.reduce_sum(st[:, 0, :], sc[:], X_AXIS))
            link(V_.reciprocal(st[:, 0, :], st[:, 0, :]))
            V_.tensor_tensor(rank[:], rank[:], bc3(st[:, 0, :], E), ALU.mult).then_inc(s["gate"], 1)
            dve.wait_ge(s["tr"], 3 * NB)
            link(V_.memset(XP[:, :, 0:K - 1], 0.0))
            dve.sem_inc(s["conv"], NH)
            dve.sem_inc(s["dtu"], 1)
            dve.sem_inc(s["bh"], 1)
            base, NL = chain[0], NH * (K - 1) + 6
            with dve.Fori(0, NB) as b:
                k = [0]

                def lnk(ins):
                    k[0] += 1
                    ins.then_inc(s["vch"], 1)
                    dve.wait_ge(s["vch"], b * NL + (base + k[0]))
                dve.wait_ge(s["pad"], b * NH + 2 * NH)
                dve.wait_ge(s["xs"], b * NH + NH)
                for h in range(NH):
                    lnk(V_.tensor_scalar(CV[:, h, :], XP[:, h, 0:L], convw_sb[:, h, 0:1], None, ALU.mult))
                    for j in range(1, K):
                        ins = V_.scalar_tensor_tensor(CV[:, h, :], XP[:, h, j:j + L], convw_sb[:, h, j:j + 1],
                                                      CV[:, h, :], ALU.mult, ALU.add)
                        lnk(ins) if j < K - 1 else ins.then_inc(s["conv"], 1)
                dve.wait_ge(s["bpp"], b + 1)
                dve.wait_ge(s["dump"], b * (16 * N_DUMP) + 16 * N_DUMP)
                lnk(V_.tensor_copy(BH[:, 0, :], ps[6][0:S, :]))
                V_.tensor_tensor(RB, ps[6][0:S, :], BH[:, 0, :], ALU.subtract).then_inc(s["bmv"], 1)
                dve.wait_ge(s["bmv"], b * 2 + 1)
                lnk(V_.tensor_copy(BH[:, 1, :], RB))
                V_.tensor_tensor(RB, RB, BH[:, 1, :], ALU.subtract).then_inc(s["bmv"], 1)
                dve.wait_ge(s["bmv"], b * 2 + 2)
                V_.tensor_copy(BH[:, 2, :], RB).then_inc(s["bh"], 1)
                dve.wait_ge(s["vexp"], b + 1)
                lnk(V_.tensor_scalar(WM, EX, 1.0, -1.0, ALU.add, ALU.add))
                lnk(V_.tensor_tensor(WM, EX, WM, ALU.subtract))
                dve.wait_ge(s["ln"], b + 2)
                lnk(V_.tensor_tensor(WM, WM, LW, ALU.add))
                flat = lambda a: a.rearrange("p h t -> p (h t)")
                lnk(V_.scalar_tensor_tensor(flat(DT), flat(V), 0.0, flat(WM), ALU.max, ALU.add))
                V_.tensor_tensor(U, DT, XS, ALU.mult).then_inc(s["dtu"], 1)
                assert k[0] == NL, (k[0], NL)

            dve.wait_ge(s["dump"], 16 * N_DUMP * (NB + 1))
            dve.sem_inc(s["scan"], TAPE)
            dve.sem_inc(s["mul"], NH)
            dve.sem_inc(s["fg"], 1)
            dve.sem_inc(s["res"], 1)
            dve.sem_inc(s["fs"], 1)
            uflat = ub.rearrange("p n h t -> p (n h t)")

            def gate_y(b):
                dve.wait_ge(s["fin"], b * (16 * N_FIN) + 16 * N_FIN)
                dve.wait_ge(s["acc"], b + 1)
                for r in range(2):
                    V_.tensor_tensor(yg[:, r, :], acc[r][:], szb[:, r, :], ALU.mult).then_inc(s["yg"], 1)
                dve.wait_ge(s["tot"], b + 1)
                dve.wait_ge(s["fgu"], b * E + (E + 1))
                V_.tensor_tensor(fS, ft[:], fsum, ALU.add).then_inc(s["fs"], 1)

            def residual(b):
                dve.wait_ge(s["wo"], b + 1)
                V_.tensor_tensor(sS, ft[:], xnb, ALU.add).then_inc(s["ss"], 1)

            def gate_s(b):
                dve.wait_ge(s["ss"], b + 1)
                dve.wait_ge(s["silu"], b + 1)
                V_.tensor_tensor(gated, gated, sS, ALU.mult).then_inc(s["gated"], 1)

            def result(b):
                dve.wait_ge(s["trf"], b + 1)
                dve.wait_ge(s["store"], b * 16 + 16)
                V_.tensor_tensor(res, ft[:].rearrange("p (j c) -> p j c", c=C), xb, ALU.add).then_inc(s["res"], 1)

            def group(b, g, slot, last=None):
                m0 = (b * E + g) * TAPE
                n0 = (b * E + g) * SG
                for i in range(SG):
                    if i == 0:
                        dve.wait_ge(s["dtl"], b * 32 + 32)
                    dve.wait_ge(s["bbc"], n0 + (i + 1))
                    for h in range(NH):
                        m = 2 * i + h
                        dve.wait_ge(s["scan"], m0 + (m + TAPE - 1))
                        V_.tensor_tensor(dBx[h][:], uflat[:, ds(slot + h * L, L)], Bbc[:],
                                         ALU.mult).then_inc(s["mul"], 1)
                    dve.wait_ge(s["prod"], n0 + (i + 1 + 2 * CG - 2))
                    for h in range(NH):
                        m = 2 * i + h
                        dve.wait_ge(s["da"], m0 + (m + 1))
                        dve.wait_ge(s["mul"], m0 + (m + 1 + NH))
                        V_.tensor_tensor_scan(hs[:, i % 2, h, :], dA[:, m, :], dBx[h][:], 0.0,
                                              ALU.mult, ALU.add).then_inc(s["scan"], 1)
                    if last is not None:
                        {1: gate_y, 2: residual, 3: gate_s, 5: result}.get(i, lambda b: None)(last)
                    if i == SG - 2:
                        dve.wait_ge(s["gl"], b * (16 * E) + g * 16 + 16)
                        dve.wait_ge(s["fgu"], b * E + g + 1)
                        dve.wait_ge(s["fo"], b * E + g + 1)
                        V_.tensor_tensor(fgate, fo[:], gateb, ALU.mult).then_inc(s["fg"], 1)

            def run(b, last):
                slot = b if isinstance(b, int) else dve.snap((b % 2) * (NH * L))
                group(b, 0, slot, last)
                with dve.Fori(1, E) as g:
                    group(b, g, slot)
            run(0, None)
            with dve.Fori(1, NB) as b:
                run(b, b - 1)
            for step in (gate_y, residual, gate_s, result):
                step(NB - 1)

        @block.tensor
        def _(pe):
            mm = nc.tensor.matmul
            pe.wait_ge(s["mask"], N_MASK)
            pe.wait_ge(s["w"], 16 * N_W)
            pe.wait_ge(s["hn"], 2)
            for b in range(NB):
                for kind, src in enumerate((XN, HN, SQX)):
                    k = 3 * b + kind
                    if k >= 8:
                        pb, pk = divmod(k - 8, 3)
                        pe.wait_ge(s["evV"], 2 * pb + (2 if pk == 2 else 1))
                        if pk:
                            pe.wait_ge(s["evA"], 2 * pb + pk)
                    for j in range(TPB):
                        ins = nc.tensor.transpose(ps[k % 8][:, j * P:(j + 1) * P], src[:, b * TPB + j, :], ident[:])
                    ins.then_inc(s["tr"], 1)
            pe.wait_ge(s["evV"], 2 * NB)
            pe.wait_ge(s["evA"], 2 * NB)
            for j in range(NT):
                ins = mm(ps[0][:, j * E:(j + 1) * E], XNT[:, j * P:(j + 1) * P], cent_sb[:], start=True, stop=True)
            ins.then_inc(s["score"], 1)
            pe.wait_ge(s["gate"], 1)
            for j in range(NT):
                ins = nc.tensor.transpose(ps[j // TPB][0:E, (j % TPB) * P:(j % TPB + 1) * P], rank[:, j, :], ident[:])
                if j % TPB == TPB - 1:
                    ins.then_inc(s["gtr"], 1)
            pe.wait_ge(s["gtc"], NB)
            with pe.Fori(0, NB) as b:
                t0 = pe.snap(b * L)
                pe.wait_ge(s["pad"], b * NH + NH)
                pe.wait_ge(s["xpz"], b + 1)
                for j in range(2 * NH):
                    mm(ps[j][:], win_sb[:, j * P:(j + 1) * P], HTT[:, ds(t0, L)], start=True, stop=True
                       ).then_inc(s["win"], 1)
                pe.wait_ge(s["ln"], b + 1)
                pe.wait_ge(s["bh"], b + 1)
                pe.wait_ge(s["cc"], b + 1)
                pe.wait_ge(s["xs"], b * NH + 2 * NH)
                for o in range(NH):
                    for h in range(NH):
                        ins = mm(ps[4 + o][:], dtw_sb[:, h, o * P:(o + 1) * P], XS[:, h, :],
                                 start=(h == 0), stop=(h == NH - 1))
                ins.then_inc(s["dtp"], 1)
                for bank, w, done in ((6, bp_sb, "bpp"), (7, cp_sb, "cpp")):
                    for h in range(NH):
                        ins = mm(ps[bank][0:S, :], w[:, h, :], XS[:, h, :], start=(h == 0), stop=(h == NH - 1))
                    ins.then_inc(s[done], 1)

            pe.wait_ge(s["dump"], 16 * N_DUMP * (NB + 1))
            pe.wait_ge(s["ln"], NB + 1)
            pe.wait_ge(s["cc"], NB + 1)
            bflat = b_parts[:].rearrange("p q t -> p (q t)")
            pflat = pick[:].rearrange("p s m -> p (s m)")
            pe.sem_inc(s["ysum"], 2)
            pe.sem_inc(s["w1u"], 1)
            pe.sem_inc(s["w2u"], 1)
            snap = lambda v: v if isinstance(v, int) else pe.snap(v)

            def open_sum(bank, stop=False):
                mm(bank[:], zrow[:, 0:P], zrow[:], start=True, stop=stop)

            def bcast(n0, i, col, sel):
                pe.wait_ge(s["mul"], n0 * 2 + (2 * i + NH))
                mm(Bbc[:], pflat[:, ds(sel, P)], bflat[:, ds(col, L)], start=True, stop=True).then_inc(s["bbc"], 1)

            def ysum(n0, i):
                pe.wait_ge(s["prod"], n0 + (i + 1 + 2 * CG))
                pe.sem_inc(s["taken"], 1)
                for r, h in ((0, 0), (1, 1), (0, 1), (1, 0)):
                    q = slice(HP * r, HP * r + HP)
                    ins = mm(acc[r][HP * h:HP * h + HP, :], ident[q, q], pr[q, i % 2, h, :], start=False, stop=False,
                             skip_group_check=True)
                ins.then_inc(s["ysum"], 1)

            def close_sums(b):
                pe.wait_ge(s["fin"], b * (16 * N_FIN) + 16 * N_FIN)
                for r in range(2):
                    ins = mm(acc[r][:], diagD[:, r, :], xsb[:, r, :], start=False, stop=True)
                ins.then_inc(s["acc"], 1)
                mm(ft[:], b2r_sb[:], gtb, start=False, stop=False)
                mm(ft[:], b2s_sb[:], ones_s[:], start=False, stop=True).then_inc(s["tot"], 1)

            def project_out(b):
                pe.wait_ge(s["fs"], b + 2)
                for r in range(2):
                    pe.wait_ge(s["yg"], b * 2 + (r + 1))
                    ins = mm(ft[:], wout_sb[:, r, :], yg[:, r, :], start=(r == 0), stop=(r == 1))
                ins.then_inc(s["wo"], 1)

            def turn_back(b):
                pe.wait_ge(s["gated"], b + 1)
                for j in range(TPB):
                    ins = nc.tensor.transpose(ft[:, j * P:(j + 1) * P], gated[:, j * P:(j + 1) * P], ident[:])
                ins.then_inc(s["trf"], 1)

            W1_AT = {0: (0, 1), 1: (2, 3), 2: (4,)}
            W2_AT = {4: (0, 1), 5: (2, 3), 6: (4,)}

            def group(b, g, t0, last=None, head=False):
                n0 = (b * E + g) * SG
                u = b * E + g
                for i in range(SG):
                    sidx = g * SG + i
                    bcast(n0, i, snap((sidx // SQ) * T + t0), snap((sidx % SQ) * P))
                    if not head or i >= 2 or last is not None:
                        if head and i == 2:
                            if last is not None:
                                pe.wait_ge(s["yg"], last * 2 + 2)
                            for r in range(2):
                                open_sum(acc[r])
                        ysum(n0, i - 2)
                    if head and i == 1 and last is not None:
                        close_sums(last)
                    if head and last is not None and i == 2:
                        project_out(last)
                    if head and last is not None and i == 5:
                        turn_back(last)
                    if head and i == SG - 2:
                        if last is not None:
                            pe.wait_ge(s["res"], last + 2)
                        open_sum(ft)
                    for t in W1_AT.get(i, ()):
                        if t == 0:
                            pe.wait_ge(s["w1l"], u * 32 + 32)
                        if t == 1:
                            pe.wait_ge(s["fg"], u + 1)
                        pe.wait_ge(s["gelu"], u * (HT + 1) + (max(t - 1, 0) + 1))
                        src = x_rr if t < HT else x_rs
                        mm(fh[t % 2][:], w1b[:, t, :], src[:, ds(t0, L)], start=True, stop=True).then_inc(s["fh"], 1)
                    if i == 3:
                        pe.wait_ge(s["fh"], (u + 1) * (HT + 1))
                        pe.sem_inc(s["w1u"], 1)
                    for t in W2_AT.get(i, ()):
                        if t == 0:
                            pe.wait_ge(s["w2l"], u * 32 + 32)
                            pe.wait_ge(s["gelu"], u * (HT + 1) + HT + 1)
                        if t < HT:
                            ins = mm(fo[:], w2b[:, t, :], hid[:, t, :], start=(t == 0), stop=(t == HT - 1))
                            if t == HT - 1:
                                ins.then_inc(s["fo"], 1)
                        else:
                            pe.wait_ge(s["gelu"], u * (HT + 1) + HT + 2)
                            mm(ft[:], w2b[:, t, :], hid[:, t, :], start=False, stop=False).then_inc(s["w2u"], 1)

            def run(b, last):
                t0 = snap(b * L)
                group(b, 0, t0, last, head=True)
                with pe.Fori(1, E) as g:
                    group(b, g, t0)
            run(0, None)
            with pe.Fori(1, NB) as b:
                run(b, b - 1)
            ysum(NB * S, -2)
            ysum(NB * S, -1)
            close_sums(NB - 1)
            project_out(NB - 1)
            turn_back(NB - 1)


N_W = 21 + 4
ARENA = 32512
N_MASK = 10
N_DUMP = 3 + 6 + 2
N_FIN = 6
EVV_XN = 16


_INS = ['L0_attn_x', 'L0_attn_norm_w', 'L0_attn_norm_b', 'L0_attn_Win', 'L0_attn_conv_w', 'L0_attn_conv_b',
        'L0_attn_dt_w', 'L0_attn_dt_b', 'L0_attn_A_log', 'L0_attn_D', 'L0_attn_Bp', 'L0_attn_Cp', 'L0_attn_Wout',
        'L0_ffn_g_shared', 'L0_ffn_W1_s', 'L0_ffn_b1_s', 'L0_ffn_W2_s', 'L0_ffn_b2_s', 'L0_ffn_g_routed',
        'L0_ffn_W1_r', 'L0_ffn_b1_r', 'L0_ffn_W2_r', 'L0_ffn_b2_r', 'L0_ffn_centroids']


def kernel(**inputs):
    import numpy as _np
    import concourse.bacc as _bacc
    from concourse import mybir as _mybir
    from concourse.bass_utils import run_bass_kernel_spmd as _run

    nc = _bacc.Bacc("TRN2", target_bir_lowering=False, num_devices=1)
    arrays, args = {}, []
    for name in _INS:
        a = _np.ascontiguousarray(inputs[name])
        arrays[f"in_{name}_dram"] = a
        args.append(nc.dram_tensor(f"in_{name}_dram", a.shape, _mybir.dt.from_np(a.dtype), kind="ExternalInput").ap())
    shape = inputs['L0_attn_x'].shape
    args.append(nc.dram_tensor("out_0_dram", shape, _mybir.dt.float32, kind="ExternalOutput").ap())
    mamba_gated_moe(nc, *args)
    r = _run(nc, [arrays], core_ids=[0])
    return r.results[0]["out_0_dram"]
```

```python
from contextlib import ExitStack

import concourse.bass as bass
from concourse import mybir

F32 = mybir.dt.float32
BF16 = mybir.dt.bfloat16
ALU = mybir.AluOpType
ACT = mybir.ActivationFunctionType
X_AXIS = mybir.AxisListType.X
ds = bass.ds

P = 128
F32_EPS = 1.1920928955078125e-07
LN_EPS = 1e-5

ARENA = 35584
N_CONSTANTS = 10
N_WEIGHTS = 21 + 4
N_BCDTU = 1 + 6 + 2
N_END = 6


def mamba_gated_moe(nc, x, norm_w, norm_b, Win, conv_w, conv_b, dt_w, dt_b, A_log, Dskip, Bp, Cp, Wout,
                    g_shared, W1_s, b1_s, W2_s, b2_s, g_routed, W1_r, b1_r, W2_r, b2_r, centroids, out):
    NB, L, C = x.shape
    T = NB * L
    NT = T // P
    TPB = L // P
    DI, S = A_log.shape
    NH = DI // P
    K = conv_w.shape[2]
    E, _, H = W1_r.shape
    ES = W1_s.shape[0]
    HT = H // P
    SG = S // E
    assert ES * HT == E == 8 and SG == 8 and HT == 4 and NH == 2 and TPB == 4 and NB == 8
    SQ = S // 2
    SCANS = 2 * SG
    HP = P // 2
    RING = 4
    LAG = 3
    PAIR = 2
    SUMMED = {0: 1, 1: 2, 2: 3, 3: 4, 4: 5, 5: 6}
    CG = SG // 2

    ctx = ExitStack()
    with ctx:
        def sb(name, shape, dt=F32):
            return ctx.enter_context(nc.sbuf_tensor(name, shape, dt))

        def sem(name):
            return ctx.enter_context(nc.semaphore(name))

        def dram(name, shape):
            return nc.dram_tensor(name, shape, F32, kind="Internal").ap()

        dt_d = dram("dt_scratch", (NH, P, T))
        u_d = dram("u_scratch", (NH, P, T))
        xs_d = dram("xs_scratch", (NH, P, T))
        sz_d = dram("sz_scratch", (NH, P, T))
        xn_d = dram("xn_scratch", (P, T))
        c_d = dram("c_scratch", (S, T))
        gate_d = dram("gate_scratch", (E, T))
        w1sh_d = dram("w1_shared_tiles", (ES * HT, C, P))
        w2sh_d = dram("w2_shared_tiles", (ES * HT, P, C))

        ident = sb("ident", [P, P])
        x_rs = sb("x_rms_shared", [P, T])
        x_rr = sb("x_rms_routed", [P, T])
        b_parts = sb("b_parts", [3 * SQ, 2, T], BF16)
        pick = sb("pick", [3 * SQ, SQ, P], BF16)
        win_sb = sb("win_sb", [P, 2 * DI])
        dtw_sb = sb("dtw_sb", [P, NH, DI])
        bp_sb = sb("bp_sb", [P, NH, S])
        cp_sb = sb("cp_sb", [P, NH, S])
        wout_sb = sb("wout_sb", [P, NH, C])
        cent_sb = sb("cent_sb", [P, E])
        neg_a = sb("neg_A", [P, NH, S])
        convw_sb = sb("convw_sb", [P, NH, K])
        vecs = sb("vecs", [P, 10])
        norm_w_col, norm_b_col, g_shared_col, g_routed_col = (vecs[:, i:i + 1] for i in range(4))
        conv_b_cols = [vecs[:, 4 + h:5 + h] for h in range(NH)]
        dt_b_cols = [vecs[:, 6 + h:7 + h] for h in range(NH)]
        d_cols = [vecs[:, 8 + h:9 + h] for h in range(NH)]
        diagD = sb("diagD", [P, NH, P])
        b1r_sb = sb("b1r_sb", [P, E * HT])
        b1s_sb = sb("b1s_sb", [P, ES * HT])
        b2r_sb = sb("b2r_sb", [E, C])
        b2s_sb = sb("b2s_sb", [ES, C])
        ones_s = sb("ones_s", [ES, L])
        zrow = sb("zrow", [1, L], BF16)
        tri = sb("tri", [P, E, E])

        TF = T
        arena = sb("arena", [P, ARENA])
        reg = [arena[:, i * TF:(i + 1) * TF] for i in range(6)]
        tok = [r.rearrange("p (j c) -> p j c", c=C) for r in reg]
        x_tok, xn_tok, square_tok, h_tok = tok[0], tok[1], tok[2], tok[3]
        xn_all, h_all = reg[0], reg[4]
        cur = [TF]

        def take(size, shape=None, **kw):
            a = arena[:, cur[0]:cur[0] + size]
            cur[0] += size
            return a.rearrange(shape, **kw) if shape else a
        conv_in = take(NH * (L + K - 1), "p (h t) -> p h t", h=NH)
        conv_out = take(NH * L, "p (h t) -> p h t", h=NH)
        silu_x_even = take(NH * L, "p (h t) -> p h t", h=NH)
        silu_z_new = take(NH * L, "p (h t) -> p h t", h=NH)
        dt_raw = take(NH * L, "p (h t) -> p h t", h=NH)
        exp_abs = take(NH * L, "p (h t) -> p h t", h=NH)
        log_w = take(NH * L, "p (h t) -> p h t", h=NH)
        log_rest = take(NH * L, "p (h t) -> p h t", h=NH)
        dt_new = take(NH * L, "p (h t) -> p h t", h=NH)
        u_new = take(NH * L, "p (h t) -> p h t", h=NH)
        b_rest = take(L)[0:S, :]
        b_new = take(3 * L // 2).bitcast(BF16).rearrange("p (k t) -> p k t", k=3)[0:S]
        c_new = take(L)[0:S, :]
        assert cur[0] <= 4 * TF
        cur[0] = 6 * TF
        scores = take(NT * E, "p (j e) -> p j e", e=E)
        rank = take(NT * E, "p (j e) -> p j e", e=E)
        stats = take(8 * NT, "p (k j) -> p k j", k=8)
        silu_x_new = (silu_x_even, take(NH * L, "p (h t) -> p h t", h=NH))
        PAIRS = (P, NT, E, E)
        same, larger = (reg[5][:, k * NT * E * E:(k + 1) * NT * E * E].rearrange("p (j a b) -> p j a b", a=E, b=E)
                        for k in range(2))
        gates_all = reg[5][0:E, :]

        cur[0] = 0
        decay = take(SCANS * L, "p (n t) -> p n t", t=L)
        c_rows = take(2 * CG * L, "p (q s t) -> p q s t", q=2, s=CG)
        silu_x_in = take(NH * L, "p (h t) -> p h t", h=NH)
        silu_z_in = take(NH * L, "p (h t) -> p h t", h=NH)
        y_gated = take(NH * L, "p (h t) -> p h t", h=NH)
        attn_sum = take(L)
        ffn_sum = take(L)
        assert cur[0] == 4 * TF
        dt_in = take(2 * NH * L, "p (n h t) -> p n h t", n=2, h=NH)
        u_in = take(2 * NH * L, "p (n h t) -> p n h t", n=2, h=NH)
        assert cur[0] == 5 * TF
        xn_in = take(L)
        x_in = take(L, "p (j c) -> p j c", c=C)
        s_times_g = take(L)
        gate_row = take(L)
        gated_expert = take(L)
        routed_sum = take(L)
        result_out = take(L, "p (j c) -> p j c", c=C)
        gates_in = take(L)[0:E, :]
        assert cur[0] == 6 * TF
        hidden = take((HT + 1) * L, "p (n t) -> p n t", t=L)
        states = take(2 * NH * L, "p (n h t) -> p n h t", n=2, h=NH)
        products = take((RING + 1) * NH * L, "p (n h t) -> p n h t", n=RING + 1, h=NH)
        w1_in = take((HT + 1) * P, "p (n k) -> p n k", k=P)
        w2_in = take((HT + 1) * P, "p (n k) -> p n k", k=P)
        assert cur[0] <= ARENA, cur[0]

        ps = [ctx.enter_context(nc.psum_tensor(f"ps{i}", [P, L], F32)) for i in range(8)]
        b_bc, u_b, y_ps, hid_ps, expert_ps, ffn_ps = ps[0], ps[1:3], ps[3:5], ps[5:7], ps[6], ps[7]

        s = {n: sem(n) for n in (
            "x_loaded0 x_loaded1 scores_compared ranks_counted pair_added weights_loaded constants_made "
            "vector_step scalar_step gpsimd_step x_centred squares_made variance_made deviation_made xn_made "
            "xn_centred h_made rms_made xn_turned h_rms_turned xn_copied h_copied expert_inputs_made "
            "scores_projected scores_ready gates_made gates_turned gates_copied gates_stored xn_stored "
            "input_projected silu_z_made conv_made silu_x_made dt_projected b_projected c_projected exp_made "
            "log_made c_copied b_split dt_u_made x_stored z_stored b_c_dt_u_stored b_rest_made conv_input_copied "
            "b_broadcast u_b_multiplied scanned decay_ready product_ready y_summed dt_u_loaded end_loaded "
            "w1_loaded w2_loaded gate_row_loaded w1_used w2_used hidden_made gelu_ready expert_made "
            "expert_gated expert_added decay_slot_claimed product_claimed xn_loaded y_complete y_gated "
            "attn_projected experts_complete ffn_sum_ready attn_sum_ready silu_ready product_s_g_ready "
            "result_turned result_ready result_stored c_rows_loaded0 c_rows_loaded1").split()}

        def turns(engine):
            with engine.Fori(0, (NB - 2) // 2) as pair:
                yield pair * 2 + 1, 1
                yield pair * 2 + 2, 0
            yield NB - 1, 1

        bc3 = lambda a, n: a.unsqueeze(2).broadcast_to((P, a.shape[1], n))

        block = ctx.enter_context(nc.Block())

        @block.sync
        def _(sp):
            sp.sem_inc(s["x_stored"], 16)
            sp.sem_inc(s["z_stored"], 16)
            sp.sem_inc(s["b_c_dt_u_stored"], 16 * N_BCDTU)
            sp.sem_inc(s["result_stored"], 16)
            for half in range(2):
                sp.dma_start(x_tok[:, half * NT // 2:(half + 1) * NT // 2, :],
                             x[half * NB // 2:(half + 1) * NB // 2].rearrange("b (j p) c -> p (b j) c", p=P)
                             ).then_inc(s[f"x_loaded{half}"], 16)
            n = 0
            for dst, src in (
                    (win_sb[:], Win), (dtw_sb[:], dt_w.rearrange("(h p) n -> p h n", p=P)),
                    (bp_sb[:], Bp.rearrange("(h p) n -> p h n", p=P)),
                    (cp_sb[:], Cp.rearrange("(h p) n -> p h n", p=P)),
                    *((wout_sb[HP * h:HP * h + HP, :, :], Wout[P * h:P * h + P].rearrange("(r q) n -> q r n", q=HP))
                      for h in range(NH)), (cent_sb[:], centroids),
                    (neg_a[:], A_log.rearrange("(h p) n -> p h n", p=P)),
                    (convw_sb[:], conv_w.rearrange("(h p) o k -> p h (o k)", p=P)),
                    (norm_w_col, norm_w.unsqueeze(1)), (norm_b_col, norm_b.unsqueeze(1)),
                    (g_shared_col, g_shared.unsqueeze(1)), (g_routed_col, g_routed.unsqueeze(1)),
                    (vecs[:, 4:6], conv_b.rearrange("(h p) -> p h", p=P)),
                    (vecs[:, 6:8], dt_b.rearrange("(h p) -> p h", p=P)),
                    *((vecs[HP * h:HP * h + HP, 8:10], Dskip[P * h:P * h + P].rearrange("(r q) -> q r", q=HP))
                      for h in range(NH)),
                    (b1r_sb[:], b1_r.rearrange("e (t p) -> p (e t)", p=P)),
                    (b1s_sb[:], b1_s.rearrange("e (t p) -> p (e t)", p=P)),
                    (b2r_sb[:], b2_r), (b2s_sb[:], b2_s)):
                with nc.allow_non_contiguous_dma(reason="small per-channel vectors"):
                    sp.dma_start(dst, src).then_inc(s["weights_loaded"], 16)
                n += 1
            for e in range(ES):
                sp.dma_start(w1sh_d[e * HT:(e + 1) * HT],
                             W1_s[e].rearrange("c (t h) -> t c h", h=P)).then_inc(s["weights_loaded"], 16)
                sp.dma_start(w2sh_d[e * HT:(e + 1) * HT],
                             W2_s[e].rearrange("(t h) c -> t h c", h=P)).then_inc(s["weights_loaded"], 16)
                n += 2
            assert n == N_WEIGHTS
            sp.wait_ge(s["xn_copied"], NB)
            sp.dma_start(xn_d, xn_all).then_inc(s["xn_stored"], 16)
            snap = lambda v: v if isinstance(v, int) else sp.snap(v)

            def store_z(b):
                t0 = snap(b * L)
                sp.wait_ge(s["silu_z_made"], b + 2)
                sp.dma_start(sz_d[:, :, ds(t0, L)].rearrange("h p t -> p h t"), silu_z_new
                                    ).then_inc(s["z_stored"], 16)

            def store_x(b, odd):
                t0 = snap(b * L)
                sp.wait_ge(s["silu_x_made"], b * NH + 2 * NH)
                sp.dma_start(xs_d[:, :, ds(t0, L)].rearrange("h p t -> p h t"), silu_x_new[odd]
                                    ).then_inc(s["x_stored"], 16)

            def store_bc(b):
                t0 = snap(b * L)
                sp.wait_ge(s["c_copied"], b + 2)
                sp.dma_start(c_d[:, ds(t0, L)], c_new).then_inc(s["b_c_dt_u_stored"], 16)
                sp.wait_ge(s["b_split"], b + 2)
                for k in range(3):
                    for q in range(2):
                        sp.dma_start(b_parts[k * SQ:(k + 1) * SQ, q, ds(t0, L)],
                                     b_new[q * SQ:(q + 1) * SQ, k, :]).then_inc(s["b_c_dt_u_stored"], 16)

            def store_dt(b):
                t0 = snap(b * L)
                sp.wait_ge(s["dt_u_made"], b + 2)
                sp.dma_start(dt_d[:, :, ds(t0, L)].rearrange("h p t -> p h t"), dt_new
                                    ).then_inc(s["b_c_dt_u_stored"], 16)
                sp.dma_start(u_d[:, :, ds(t0, L)].rearrange("h p t -> p h t"), u_new
                                    ).then_inc(s["b_c_dt_u_stored"], 16)

            store_z(0)
            store_x(0, 0)
            for b, odd in turns(sp):
                store_z(b)
                store_bc(b - 1)
                store_x(b, odd)
                store_dt(b - 1)
            sp.wait_ge(s["input_projected"], 4 * NB)
            sp.wait_ge(s["b_c_dt_u_stored"], 16 * N_BCDTU * 2)
            for dst, src in ((dt_in, dt_d), (u_in, u_d)):
                sp.dma_start(dst[:, 0, :, :], src[:, :, 0:L].rearrange("h p t -> p h t")
                                    ).then_inc(s["dt_u_loaded"], 16)
            store_bc(NB - 1)
            sp.wait_ge(s["weights_loaded"], 16 * N_WEIGHTS)

            def load_c(b, g, half):
                srow = snap(g * SG + half * CG)
                tb = snap(b * L)
                sp.wait_ge(s["product_ready"], (b * S + g * SG) + (half * CG + CG))
                sp.dma_start(c_rows[:, half, :, :],
                             c_d[ds(srow, CG), ds(tb, L)].unsqueeze(0).broadcast_to((P, CG, L))
                             ).then_inc(s[f"c_rows_loaded{half}"], 16)

            def load_w1(b, g):
                sp.wait_ge(s["w1_used"], b * E + g + 1)
                sp.dma_start(w1_in[:, 0:HT, :].rearrange("p n k -> p (n k)"),
                             W1_r[ds(g, 1)].rearrange("e c h -> (e c) h")).then_inc(s["w1_loaded"], 16)
                sp.dma_start(w1_in[:, HT, :], w1sh_d[ds(g, 1)].rearrange("e c h -> (e c) h")
                             ).then_inc(s["w1_loaded"], 16)

            def load_w2(b, g):
                sp.wait_ge(s["w2_used"], b * E + g + 1)
                sp.dma_start(w2_in[:, 0:HT, :],
                             W2_r[ds(g, 1)].rearrange("e (t h) c -> (e h) t c", h=P)).then_inc(s["w2_loaded"], 16)
                sp.dma_start(w2_in[:, HT, :], w2sh_d[ds(g, 1)].rearrange("e h c -> (e h) c")
                             ).then_inc(s["w2_loaded"], 16)

            def load_gate(b, g):
                tb = snap(b * L)
                sp.wait_ge(s["expert_gated"], b * E + g + 1)
                sp.dma_start(gate_row, gate_d[ds(g, 1), ds(tb, L)].broadcast_to((P, L))
                             ).then_inc(s["gate_row_loaded"], 16)

            def load_group(b, g):
                load_c(b, g, 0)
                load_w1(b, g)
                load_c(b, g, 1)
                load_w2(b, g)
                load_gate(b, g)

            load_w1(0, 0)
            load_w2(0, 0)
            sp.wait_ge(s["dt_u_made"], NB + 1)
            load_c(0, 0, 0)
            load_c(0, 0, 1)
            store_dt(NB - 1)
            sp.wait_ge(s["gates_copied"], NB)
            sp.dma_start(gate_d, gates_all).then_inc(s["gates_stored"], 16)
            sp.wait_ge(s["gates_stored"], 16)
            load_gate(0, 0)
            sp.wait_ge(s["x_stored"], 16 * (NB + 1))
            sp.wait_ge(s["z_stored"], 16 * (NB + 1))
            sp.wait_ge(s["b_c_dt_u_stored"], 16 * N_BCDTU * (NB + 1))
            sp.wait_ge(s["xn_stored"], 16)

            def store_result(b):
                row = snap(b + 0)
                sp.wait_ge(s["result_ready"], b + 2)
                sp.dma_start(out[ds(row, 1)].rearrange("b (j p) c -> p (b j) c", p=P), result_out
                             ).then_inc(s["result_stored"], 16)

            def load_block(b, first):
                if not first:
                    load_group(b, 0)
                nb = snap(((b + 1) % NB) * L)
                slot = snap(((b + 1) % 2) * (NH * L))
                sp.wait_ge(s["scanned"], b * (2 * S) + SCANS)
                sp.wait_ge(s["dt_u_loaded"], b * 32 + 32)
                for dst, src in ((dt_in, dt_d), (u_in, u_d)):
                    flat = dst.rearrange("p n h t -> p (n h t)")
                    sp.dma_start(flat[:, ds(slot, NH * L)].rearrange("p (h t) -> p h t", h=NH),
                                 src[:, :, ds(nb, L)].rearrange("h p t -> p h t")).then_inc(s["dt_u_loaded"], 16)
                tb = snap(b * L)
                if not first:
                    sp.wait_ge(s["attn_sum_ready"], b + 0)
                sp.dma_start(xn_in, xn_d[:, ds(tb, L)]).then_inc(s["xn_loaded"], 16)
                with sp.Fori(1, E) as g:
                    load_group(b, g)
                if not first:
                    store_result(b - 1)
                row = snap(b + 0)
                sp.wait_ge(s["result_ready"], b + 1)
                for dst, src in ((silu_x_in, xs_d), (silu_z_in, sz_d)):
                    for h in range(NH):
                        sp.dma_start(dst[HP * h:HP * h + HP, :, :],
                                     src[h, :, ds(tb, L)].rearrange("(r q) t -> q r t", q=HP)
                                                         ).then_inc(s["end_loaded"], 16)
                sp.dma_start(gates_in, gate_d[:, ds(tb, L)]).then_inc(s["end_loaded"], 16)
                sp.dma_start(x_in, x[ds(row, 1)].rearrange("b (j p) c -> p (b j) c", p=P)
                                    ).then_inc(s["end_loaded"], 16)

            load_block(0, True)
            with sp.Fori(1, NB) as b:
                load_block(b, False)
            store_result(NB - 1)
            sp.wait_ge(s["result_stored"], 16 * NB + 16)
            sp.wait_ge(s["dt_u_loaded"], 32 * (NB + 1))

        @block.gpsimd
        def _(pool):
            m = s["constants_made"]
            nc.gpsimd.memset(ident[:], 0.0).then_inc(m, 1)
            nc.gpsimd.memset(pick[:], 0.0).then_inc(m, 1)
            nc.gpsimd.memset(tri[:], 1.0).then_inc(m, 1)
            pool.wait_ge(m, 3)
            nc.gpsimd.affine_select(out=ident[:], in_=ident[:], compare_op=ALU.not_equal, fill=1.0, base=0,
                                    pattern=[[-1, P]], channel_multiplier=1).then_inc(m, 1)
            for k in range(3):
                nc.gpsimd.affine_select(out=pick[:], in_=pick[:], compare_op=ALU.not_equal, fill=1.0, base=-k * SQ,
                                        pattern=[[-1, SQ], [0, P]], channel_multiplier=1).then_inc(m, 1)
                pool.wait_ge(m, 5 + k)
            nc.gpsimd.affine_select(out=tri[:], in_=tri[:], compare_op=ALU.is_gt, fill=0.0, base=0,
                                    pattern=[[1, E], [-1, E]], channel_multiplier=0).then_inc(m, 1)
            nc.gpsimd.memset(ones_s[:], 1.0).then_inc(m, 1)
            nc.gpsimd.memset(zrow[:], 0.0).then_inc(m, 1)
            links = [0]

            def link(ins):
                links[0] += 1
                ins.then_inc(s["gpsimd_step"], 1)
                pool.wait_ge(s["gpsimd_step"], links[0])
            tt = nc.gpsimd.tensor_tensor
            pool.wait_ge(m, N_CONSTANTS)
            pool.wait_ge(s["scores_compared"], 2)
            link(tt(same, same, tri[:].unsqueeze(1).broadcast_to(PAIRS), ALU.mult))
            link(tt(same, same, larger, ALU.add))
            link(tt(larger[:, :, :, 0:4], same[:, :, :, 0:4], same[:, :, :, 4:8], ALU.add))
            link(tt(same[:, :, :, 0:2], larger[:, :, :, 0:2], larger[:, :, :, 2:4], ALU.add))
            tt(rank, same[:, :, :, 0], same[:, :, :, 1], ALU.add).then_inc(s["ranks_counted"], 1)
            link(tt(larger[:, :, 0, 0:4], scores[:, :, 0:4], scores[:, :, 4:8], ALU.add))
            link(tt(larger[:, :, 1, 0:2], larger[:, :, 0, 0:2], larger[:, :, 0, 2:4], ALU.add))
            tt(stats[:, 0, :], larger[:, :, 1, 0], larger[:, :, 1, 1], ALU.add).then_inc(s["ranks_counted"], 1)
            pool.drain().then_inc(s["product_ready"], 2 * CG)
            pool.sem_inc(s["expert_added"], 1)

            def group(b, g, head=False):
                u = b * E + g
                for i in range(SG):
                    n = b * S + g * SG
                    if i % CG == 0:
                        pool.wait_ge(s[f"c_rows_loaded{i // CG}"], (b * E + g + 1) * 16)
                    if i == SG - 1:
                        pool.wait_ge(s["expert_gated"], b * E + g + 2)
                        if head:
                            pool.wait_ge(s["ffn_sum_ready"], b + 1)
                            pool.wait_ge(s["xn_loaded"], b * 16 + 16)
                            nc.gpsimd.tensor_tensor(routed_sum, xn_in, gated_expert, ALU.add
                                                ).then_inc(s["expert_added"], 1)
                        else:
                            pool.wait_ge(s["expert_added"], b * E + g + 1)
                            nc.gpsimd.tensor_tensor(routed_sum, routed_sum, gated_expert, ALU.add
                                                ).then_inc(s["expert_added"], 1)
                    if i in (PAIR + RING, PAIR + 1 + RING):
                        pool.wait_ge(s["pair_added"], u + 1)
                    else:
                        pool.wait_ge(s["y_summed"], u * (SG - 1) + SUMMED[i])
                    pool.wait_ge(s["scanned"], n * 2 + (SCANS + 2 * i + 2))
                    nc.gpsimd.tensor_tensor(
                        products[:, i % RING, :, :], states[:, i % 2, :, :],
                        c_rows[:, i // CG, i % CG, :].unsqueeze(1).broadcast_to((P, NH, L)),
                        ALU.mult).then_inc(s["product_ready"], 1)
                    if i == PAIR + 1:
                        pool.wait_ge(s["product_ready"], n + (i + 1 + 2 * CG))
                        nc.gpsimd.tensor_tensor(products[:, RING, :, :], products[:, PAIR, :, :],
                                                products[:, PAIR + 1, :, :], ALU.add).then_inc(s["pair_added"], 1)

            with pool.Fori(0, NB) as b:
                group(b, 0, head=True)
                with pool.Fori(1, E) as g:
                    group(b, g)

        @block.scalar
        def _(act):
            chain = [0]

            def link(ins):
                chain[0] += 1
                ins.then_inc(s["scalar_step"], 1)
                act.wait_ge(s["scalar_step"], chain[0])

            act.wait_ge(s["weights_loaded"], 16 * N_WEIGHTS)
            link(nc.scalar.activation(neg_a[:], neg_a[:], ACT.Exp))
            link(nc.scalar.activation(neg_a[:], neg_a[:], ACT.Copy, scale=-1.0))
            half = [slice(k * NT // 2, (k + 1) * NT // 2) for k in range(2)]
            for k in range(2):
                act.wait_ge(s["x_centred"], k + 1)
                nc.scalar.activation(square_tok[:, half[k], :], xn_tok[:, half[k], :], ACT.Square
                                    ).then_inc(s["squares_made"], 1)
            for k in range(2):
                act.wait_ge(s["variance_made"], k + 1)
                nc.scalar.activation(stats[:, 2, half[k]], stats[:, 1, half[k]], ACT.Sqrt
                                    ).then_inc(s["deviation_made"], 1)
            for k in range(2):
                act.wait_ge(s["xn_centred"], k + 1)
                nc.scalar.activation(square_tok[:, half[k], :], h_tok[:, half[k], :], ACT.Square
                                    ).then_inc(s["squares_made"], 1)
            for k in range(2):
                act.wait_ge(s["variance_made"], k + 3)
                nc.scalar.activation(stats[:, 6:8, half[k]], stats[:, 4:6, half[k]], ACT.Sqrt
                                    ).then_inc(s["deviation_made"], 1)
            for b in range(NB):
                act.wait_ge(s["xn_turned"], b + 1)
                nc.scalar.copy(xn_all[:, b * L:(b + 1) * L], ps[b][:]).then_inc(s["xn_copied"], 1)
            for b in range(NB):
                act.wait_ge(s["h_rms_turned"], 2 * b + 1)
                nc.scalar.activation(h_all[:, b * L:(b + 1) * L], ps[2 * b % 8][:], ACT.Identity,
                                     scale=norm_w_col, bias=norm_b_col).then_inc(s["h_copied"], 1)
            base = chain[0]
            NL = 2
            for name, free in (("silu_x_made", NH), ("conv_input_copied", NH), ("silu_z_made", 1), ("log_made", 1),
                               ("c_copied", 1)):
                act.sem_inc(s[name], free)

            def pad(b):
                act.wait_ge(s["input_projected"], b * 4 + 2)
                act.wait_ge(s["conv_made"], b * NH + NH)
                for h in range(NH):
                    nc.scalar.copy(conv_in[:, h, K - 1:K - 1 + L], ps[h][:]).then_inc(s["conv_input_copied"], 1)

            def silu_z(b):
                act.wait_ge(s["input_projected"], b * 4 + 4)
                act.wait_ge(s["z_stored"], b * 16 + 16)
                for h in range(NH):
                    ins = nc.scalar.activation(silu_z_new[:, h, :], ps[NH + h][:], ACT.Silu)
                ins.then_inc(s["silu_z_made"], 1)

            def silu_x(b, odd):
                if not isinstance(b, int):
                    act.wait_ge(s["dt_u_made"], b + 0)
                    act.wait_ge(s["x_stored"], b * 16)
                for h in range(NH):
                    act.wait_ge(s["conv_made"], b * NH + (NH + h + 1))
                    nc.scalar.activation(silu_x_new[odd][:, h, :], conv_out[:, h, :], ACT.Silu, bias=conv_b_cols[h]
                                        ).then_inc(s["silu_x_made"], 1)

            def softplus_parts(b):
                def lnk(ins, k):
                    ins.then_inc(s["scalar_step"], 1)
                    act.wait_ge(s["scalar_step"], b * NL + (base + k))
                act.wait_ge(s["dt_projected"], b + 1)
                act.wait_ge(s["dt_u_made"], b + 1)
                nc.scalar.activation(dt_raw[:, 0, :], ps[4][:], ACT.Identity, bias=dt_b_cols[0])
                lnk(nc.scalar.activation(dt_raw[:, 1, :], ps[5][:], ACT.Identity, bias=dt_b_cols[1]), 1)
                lnk(nc.scalar.activation(exp_abs, dt_raw, ACT.Abs), 2)
                nc.scalar.activation(exp_abs, exp_abs, ACT.Exp, scale=-1.0).then_inc(s["exp_made"], 1)
                act.wait_ge(s["exp_made"], b + 1)
                nc.scalar.activation(log_w, exp_abs, ACT.Ln, bias=1.0).then_inc(s["log_made"], 1)
                act.wait_ge(s["c_projected"], b + 1)
                act.wait_ge(s["b_c_dt_u_stored"], b * (16 * N_BCDTU) + 16 * N_BCDTU)
                nc.scalar.copy(c_new, ps[7][0:S, :]).then_inc(s["c_copied"], 1)

            pad(0)
            silu_z(0)
            silu_x(0, 0)
            act.wait_ge(s["scores_projected"], 1)
            nc.scalar.activation(scores.rearrange("p j e -> p (j e)"), ps[4][:, 0:NT * E], ACT.Sigmoid
                                ).then_inc(s["scores_ready"], 1)
            for b, odd in turns(act):
                pad(b)
                silu_z(b)
                softplus_parts(b - 1)
                silu_x(b, odd)

            def copy_gates(blocks):
                for b in blocks:
                    act.wait_ge(s["gates_turned"], b + 1)
                    nc.scalar.copy(gates_all[:, b * L:(b + 1) * L], ps[b % 4][0:E, :]).then_inc(s["gates_copied"], 1)

            copy_gates(range(4))
            softplus_parts(NB - 1)
            copy_gates(range(4, NB))

            act.sem_inc(s["gelu_ready"], 1)
            act.wait_ge(s["xn_stored"], 16)
            dflat = dt_in.rearrange("p n h t -> p (n h t)")
            aflat = neg_a[:].rearrange("p h s -> p (h s)")

            snap = lambda v: v if isinstance(v, int) else act.snap(v)

            def group(b, g, slot, last=None, first=False):
                u = b * E + g
                m0 = (b * E + g) * SCANS
                for i in range(SG):
                    if first and i == SG // 2:
                        act.wait_ge(s["x_stored"], 16 * (NB + 1))
                        act.wait_ge(s["z_stored"], 16 * (NB + 1))
                        act.wait_ge(s["dt_u_made"], NB + 1)
                        hidden_tiles(b, g, u)
                    for h in range(NH):
                        act.wait_ge(s["scanned"], m0 + (2 * i + h + 1))
                        act.sem_inc(s["decay_slot_claimed"], 1)
                        col = snap(g * SG + (h * S + i))
                        nc.scalar.activation(decay[:, 2 * i + h, :], dflat[:, ds(slot + h * L, L)], ACT.Exp,
                                             scale=aflat[:, ds(col, 1)]).then_inc(s["decay_ready"], 1)
                if not first:
                    hidden_tiles(b, g, u, last)

            def hidden_tiles(b, g, u, last=None):
                act.wait_ge(s["w2_used"], u + 1)
                for t in range(HT + 1):
                    if t == HT and last is not None:
                        silu_of(last)
                    bias = b1r_sb[:, ds(g * HT + t, 1)] if t < HT else b1s_sb[:, ds(g, 1)]
                    act.wait_ge(s["hidden_made"], u * (HT + 1) + (t + 1))
                    act.wait_ge(s["weights_loaded"], 16 * N_WEIGHTS)
                    nc.scalar.activation(hidden[:, t, :], hid_ps[t % 2][:], ACT.Gelu, bias=bias
                                        ).then_inc(s["gelu_ready"], 1)

            def silu_of(b):
                act.wait_ge(s["ffn_sum_ready"], b + 2)
                nc.scalar.activation(s_times_g, ffn_sum, ACT.Silu).then_inc(s["silu_ready"], 1)

            def run(b, last):
                slot = b if isinstance(b, int) else act.snap((b % 2) * (NH * L))
                act.wait_ge(s["dt_u_loaded"], b * 32 + 32)
                group(b, 0, slot, last, first=last is None)
                with act.Fori(1, E) as g:
                    group(b, g, slot)
            run(0, None)
            with act.Fori(1, NB) as b:
                run(b, b - 1)
            silu_of(NB - 1)

        @block.vector
        def _(dve):
            chain = [0]

            def link(ins):
                chain[0] += 1
                ins.then_inc(s["vector_step"], 1)
                dve.wait_ge(s["vector_step"], chain[0])
            vector = nc.vector
            half = [slice(k * NT // 2, (k + 1) * NT // 2) for k in range(2)]
            for k, j in enumerate(half):
                dve.wait_ge(s[f"x_loaded{k}"], 16)
                link(vector.reduce_sum(stats[:, 0, j], x_tok[:, j, :], X_AXIS))
                link(vector.tensor_scalar(stats[:, 0, j], stats[:, 0, j], 1.0 / C, None, ALU.mult))
                vector.tensor_tensor(xn_tok[:, j, :], x_tok[:, j, :], bc3(stats[:, 0, j], C), ALU.subtract
                                    ).then_inc(s["x_centred"], 1)
            for k, j in enumerate(half):
                dve.wait_ge(s["squares_made"], k + 1)
                link(vector.reduce_sum(stats[:, 1, j], square_tok[:, j, :], X_AXIS))
                vector.tensor_scalar(stats[:, 1, j], stats[:, 1, j], 1.0 / C, LN_EPS, ALU.mult, ALU.add
                                    ).then_inc(s["variance_made"], 1)
            for k, j in enumerate(half):
                dve.wait_ge(s["deviation_made"], k + 1)
                link(vector.reciprocal(stats[:, 2, j], stats[:, 2, j]))
                vector.tensor_tensor(xn_tok[:, j, :], xn_tok[:, j, :], bc3(stats[:, 2, j], C), ALU.mult
                                    ).then_inc(s["xn_made"], 1)
            for k, j in enumerate(half):
                dve.wait_ge(s["xn_made"], k + 1)
                link(vector.reduce_sum(stats[:, 3, j], xn_tok[:, j, :], X_AXIS))
                link(vector.tensor_scalar(stats[:, 3, j], stats[:, 3, j], 1.0 / C, None, ALU.mult))
                vector.tensor_tensor(h_tok[:, j, :], xn_tok[:, j, :], bc3(stats[:, 3, j], C), ALU.subtract
                                    ).then_inc(s["xn_centred"], 1)
            for k, j in enumerate(half):
                dve.wait_ge(s["squares_made"], k + 3)
                link(vector.reduce_sum(stats[:, 4, j], square_tok[:, j, :], X_AXIS))
                link(vector.tensor_scalar(stats[:, 4, j], stats[:, 4, j], 1.0 / C, None, ALU.mult))
                link(vector.tensor_tensor(stats[:, 5, j], stats[:, 3, j], stats[:, 3, j], ALU.mult))
                link(vector.scalar_tensor_tensor(stats[:, 5, j], stats[:, 5, j], F32_EPS, stats[:, 4, j],
                                                 ALU.add, ALU.add))
                vector.tensor_scalar(stats[:, 4, j], stats[:, 4, j], LN_EPS, None, ALU.add
                                    ).then_inc(s["variance_made"], 1)
            for k, j in enumerate(half):
                dve.wait_ge(s["deviation_made"], k + 3)
                link(vector.reciprocal(stats[:, 6:8, j], stats[:, 6:8, j]))
                vector.tensor_tensor(h_tok[:, j, :], h_tok[:, j, :], bc3(stats[:, 6, j], C), ALU.mult
                                    ).then_inc(s["h_made"], 1)
                vector.tensor_tensor(square_tok[:, j, :], xn_tok[:, j, :], bc3(stats[:, 7, j], C), ALU.mult
                                    ).then_inc(s["rms_made"], 1)
            dve.wait_ge(s["weights_loaded"], 16 * N_WEIGHTS)
            for b in range(NB):
                dve.wait_ge(s["h_rms_turned"], 2 * b + 2)
                for dst, g in ((x_rr, g_routed_col), (x_rs, g_shared_col)):
                    ins = vector.tensor_scalar(dst[:, b * L:(b + 1) * L], ps[(2 * b + 1) % 8][:], g, None, ALU.mult)
                ins.then_inc(s["expert_inputs_made"], 1)
            dve.wait_ge(s["constants_made"], N_CONSTANTS)
            for h in range(NH):
                vector.tensor_scalar(diagD[:, h, :], ident[:], d_cols[h], None, ALU.mult
                                    ).then_inc(s["expert_inputs_made"], 1)
            link(vector.memset(conv_in[:, :, 0:K - 1], 0.0))
            dve.sem_inc(s["conv_made"], NH)
            dve.sem_inc(s["dt_u_made"], 1)
            dve.sem_inc(s["b_split"], 1)
            flat = lambda a: a.rearrange("p h t -> p (h t)")
            NCONV, NSOFT = NH * (K - 1), 6

            def convolve(b, done):
                k = 0
                dve.wait_ge(s["conv_input_copied"], b * NH + 2 * NH)
                for h in range(NH):
                    dve.wait_ge(s["silu_x_made"], b * NH + (h + 1))
                    ins = vector.tensor_scalar(conv_out[:, h, :], conv_in[:, h, 0:L], convw_sb[:, h, 0:1], None,
                                               ALU.mult)
                    for j in range(1, K):
                        k += 1
                        ins.then_inc(s["vector_step"], 1)
                        dve.wait_ge(s["vector_step"], done + k)
                        ins = vector.scalar_tensor_tensor(conv_out[:, h, :], conv_in[:, h, j:j + L],
                                                          convw_sb[:, h, j:j + 1],
                                                      conv_out[:, h, :], ALU.mult, ALU.add)
                    ins.then_inc(s["conv_made"], 1)

            def parts_and_dt(b, odd, done):
                k = [0]

                def lnk(ins):
                    k[0] += 1
                    ins.then_inc(s["vector_step"], 1)
                    dve.wait_ge(s["vector_step"], done + k[0])
                dve.wait_ge(s["b_projected"], b + 1)
                dve.wait_ge(s["b_c_dt_u_stored"], b * (16 * N_BCDTU) + 16 * N_BCDTU)
                lnk(vector.tensor_copy(b_new[:, 0, :], ps[6][0:S, :]))
                vector.tensor_tensor(b_rest, ps[6][0:S, :], b_new[:, 0, :], ALU.subtract
                                    ).then_inc(s["b_rest_made"], 1)
                dve.wait_ge(s["b_rest_made"], b * 2 + 1)
                lnk(vector.tensor_copy(b_new[:, 1, :], b_rest))
                vector.tensor_tensor(b_rest, b_rest, b_new[:, 1, :], ALU.subtract).then_inc(s["b_rest_made"], 1)
                dve.wait_ge(s["b_rest_made"], b * 2 + 2)
                vector.tensor_copy(b_new[:, 2, :], b_rest).then_inc(s["b_split"], 1)
                dve.wait_ge(s["exp_made"], b + 1)
                lnk(vector.tensor_scalar(log_rest, exp_abs, 1.0, -1.0, ALU.add, ALU.add))
                lnk(vector.tensor_tensor(log_rest, exp_abs, log_rest, ALU.subtract))
                dve.wait_ge(s["log_made"], b + 2)
                lnk(vector.tensor_tensor(log_rest, log_rest, log_w, ALU.add))
                lnk(vector.scalar_tensor_tensor(flat(dt_new), flat(dt_raw), 0.0, flat(log_rest), ALU.max, ALU.add))
                vector.tensor_tensor(u_new, dt_new, silu_x_new[odd], ALU.mult).then_inc(s["dt_u_made"], 1)
                assert k[0] == NSOFT, k[0]

            base, NL = chain[0], NCONV + NSOFT
            convolve(0, base)
            dve.wait_ge(s["scores_ready"], 1)
            other = scores.unsqueeze(2).broadcast_to(PAIRS)
            own = scores.unsqueeze(3).broadcast_to(PAIRS)
            vector.tensor_tensor(same, other, own, ALU.is_equal).then_inc(s["scores_compared"], 1)
            vector.tensor_tensor(larger, other, own, ALU.is_gt).then_inc(s["scores_compared"], 1)
            for b, odd in turns(dve):
                convolve(b, b * NL + (base + NCONV - NL))
                parts_and_dt(b - 1, 1 - odd, b * NL + (base + 2 * NCONV - NL))
            done = base + NCONV + (NB - 1) * NL
            dve.wait_ge(s["ranks_counted"], 2)
            vector.scalar_tensor_tensor(rank.rearrange("p j e -> p (j e)"), rank.rearrange("p j e -> p (j e)"),
                                    1.5, scores.rearrange("p j e -> p (j e)"), ALU.is_lt, ALU.mult
                                                        ).then_inc(s["vector_step"], 1)
            vector.reciprocal(stats[:, 0, :], stats[:, 0, :]).then_inc(s["vector_step"], 1)
            dve.wait_ge(s["vector_step"], done + 2)
            vector.tensor_tensor(rank, rank, bc3(stats[:, 0, :], E), ALU.mult).then_inc(s["gates_made"], 1)
            parts_and_dt(NB - 1, (NB - 1) % 2, done + 2)

            dve.sem_inc(s["scanned"], SCANS)
            dve.sem_inc(s["u_b_multiplied"], NH)
            dve.sem_inc(s["expert_gated"], 1)
            dve.sem_inc(s["result_ready"], 1)
            dve.sem_inc(s["ffn_sum_ready"], 1)
            uflat = u_in.rearrange("p n h t -> p (n h t)")

            def gate_y(b):
                dve.wait_ge(s["end_loaded"], b * (16 * N_END) + 16 * N_END)
                dve.wait_ge(s["y_complete"], b + 1)
                for r in range(2):
                    vector.tensor_tensor(y_gated[:, r, :], y_ps[r][:], silu_z_in[:, r, :], ALU.mult
                                        ).then_inc(s["y_gated"], 1)
                dve.wait_ge(s["experts_complete"], b + 1)
                dve.wait_ge(s["expert_added"], b * E + (E + 1))
                vector.tensor_tensor(ffn_sum, ffn_ps[:], routed_sum, ALU.add).then_inc(s["ffn_sum_ready"], 1)

            def residual(b):
                dve.wait_ge(s["attn_projected"], b + 1)
                vector.tensor_tensor(attn_sum, ffn_ps[:], xn_in, ALU.add).then_inc(s["attn_sum_ready"], 1)

            def gate_s(b):
                dve.wait_ge(s["attn_sum_ready"], b + 1)
                dve.wait_ge(s["silu_ready"], b + 1)
                vector.tensor_tensor(s_times_g, s_times_g, attn_sum, ALU.mult).then_inc(s["product_s_g_ready"], 1)

            def result(b):
                dve.wait_ge(s["result_turned"], b + 1)
                dve.wait_ge(s["result_stored"], b * 16 + 16)
                vector.tensor_tensor(result_out, ffn_ps[:].rearrange("p (j c) -> p j c", c=C), x_in, ALU.add
                                    ).then_inc(s["result_ready"], 1)

            def group(b, g, slot, last=None):
                m0 = (b * E + g) * SCANS
                n0 = (b * E + g) * SG
                for i in range(SG):
                    if i == 0:
                        dve.wait_ge(s["dt_u_loaded"], b * 32 + 32)
                    dve.wait_ge(s["b_broadcast"], n0 + (i + 1))
                    for h in range(NH):
                        m = 2 * i + h
                        dve.wait_ge(s["scanned"], m0 + (m + SCANS - 1))
                        vector.tensor_tensor(u_b[h][:], uflat[:, ds(slot + h * L, L)], b_bc[:],
                                         ALU.mult).then_inc(s["u_b_multiplied"], 1)
                    dve.wait_ge(s["product_ready"], n0 + (i + 1 + 2 * CG - 2))
                    for h in range(NH):
                        m = 2 * i + h
                        dve.wait_ge(s["decay_ready"], m0 + (m + 1))
                        dve.wait_ge(s["u_b_multiplied"], m0 + (m + 1 + NH))
                        vector.tensor_tensor_scan(states[:, i % 2, h, :], decay[:, m, :], u_b[h][:], 0.0,
                                              ALU.mult, ALU.add).then_inc(s["scanned"], 1)
                    if last is not None:
                        {2: gate_y, 3: residual, 5: gate_s, 6: result}.get(i, lambda b: None)(last)
                    if i == SG - 2:
                        dve.wait_ge(s["gate_row_loaded"], b * (16 * E) + g * 16 + 16)
                        dve.wait_ge(s["expert_added"], b * E + g + 1)
                        dve.wait_ge(s["expert_made"], b * E + g + 1)
                        vector.tensor_tensor(gated_expert, expert_ps[:], gate_row, ALU.mult
                                            ).then_inc(s["expert_gated"], 1)

            def run(b, last):
                slot = b if isinstance(b, int) else dve.snap((b % 2) * (NH * L))
                group(b, 0, slot, last)
                with dve.Fori(1, E) as g:
                    group(b, g, slot)
            run(0, None)
            with dve.Fori(1, NB) as b:
                run(b, b - 1)
            for step in (gate_y, residual, gate_s, result):
                step(NB - 1)

        @block.tensor
        def _(pe):
            mm = nc.tensor.matmul
            pe.sem_inc(s["w1_used"], 1)
            pe.sem_inc(s["w2_used"], 1)
            pe.wait_ge(s["constants_made"], N_CONSTANTS)
            pe.wait_ge(s["weights_loaded"], 16 * N_WEIGHTS)
            snap = lambda v: v if isinstance(v, int) else pe.snap(v)

            def turn(bank, src, b):
                for j in range(TPB):
                    ins = nc.tensor.transpose(bank[:, j * P:(j + 1) * P], src[:, b * TPB + j, :], ident[:])
                return ins

            for b in range(NB):
                pe.wait_ge(s["xn_made"], 1 + b // (NB // 2))
                turn(ps[b], xn_tok, b).then_inc(s["xn_turned"], 1)
            for b in range(NB):
                if b < 4:
                    pe.wait_ge(s["xn_copied"], 2 * b + 2)
                else:
                    pe.wait_ge(s["h_copied"], b - 3)
                    pe.wait_ge(s["expert_inputs_made"], b - 3)
                pe.wait_ge(s["h_made"], 1 + b // (NB // 2))
                turn(ps[2 * b % 8], h_tok, b).then_inc(s["h_rms_turned"], 1)
                pe.wait_ge(s["rms_made"], 1 + b // (NB // 2))
                turn(ps[(2 * b + 1) % 8], square_tok, b).then_inc(s["h_rms_turned"], 1)
            pe.wait_ge(s["h_copied"], NB)
            pe.wait_ge(s["expert_inputs_made"], NB)

            def project_in(b):
                t0 = snap(b * L)
                pe.wait_ge(s["conv_input_copied"], b * NH + NH)
                pe.wait_ge(s["silu_z_made"], b + 1)
                for j in range(2 * NH):
                    mm(ps[j][:], win_sb[:, j * P:(j + 1) * P], h_all[:, ds(t0, L)], start=True, stop=True
                       ).then_inc(s["input_projected"], 1)

            def project_dt_b_c(b, odd):
                pe.wait_ge(s["log_made"], b + 1)
                pe.wait_ge(s["b_split"], b + 1)
                pe.wait_ge(s["c_copied"], b + 1)
                pe.wait_ge(s["silu_x_made"], b * NH + 2 * NH)
                for o in range(NH):
                    for h in range(NH):
                        ins = mm(ps[4 + o][:], dtw_sb[:, h, o * P:(o + 1) * P], silu_x_new[odd][:, h, :],
                                 start=(h == 0), stop=(h == NH - 1))
                ins.then_inc(s["dt_projected"], 1)
                for bank, w, done in ((6, bp_sb, "b_projected"), (7, cp_sb, "c_projected")):
                    for h in range(NH):
                        ins = mm(ps[bank][0:S, :], w[:, h, :], silu_x_new[odd][:, h, :],
                                 start=(h == 0), stop=(h == NH - 1))
                    ins.then_inc(s[done], 1)

            project_in(0)
            for j in range(NT):
                ins = mm(ps[4][:, j * E:(j + 1) * E], xn_all[:, j * P:(j + 1) * P], cent_sb[:], start=True, stop=True)
            ins.then_inc(s["scores_projected"], 1)
            pe.wait_ge(s["scores_ready"], 1)
            for b, odd in turns(pe):
                project_in(b)
                project_dt_b_c(b - 1, 1 - odd)

            def turn_gates(blocks):
                for b in blocks:
                    if b >= 4:
                        pe.wait_ge(s["gates_copied"], b - 3)
                    for j in range(TPB):
                        ins = nc.tensor.transpose(ps[b % 4][0:E, j * P:(j + 1) * P], rank[:, b * TPB + j, :], ident[:])
                    ins.then_inc(s["gates_turned"], 1)

            pe.wait_ge(s["gates_made"], 1)
            pe.wait_ge(s["conv_input_copied"], NB * NH + NH)
            pe.wait_ge(s["silu_z_made"], NB + 1)
            turn_gates(range(4))
            project_dt_b_c(NB - 1, (NB - 1) % 2)
            turn_gates(range(4, NB))

            pe.wait_ge(s["b_c_dt_u_stored"], 16 * N_BCDTU * 2)
            pe.wait_ge(s["gates_copied"], NB)
            pe.wait_ge(s["log_made"], NB + 1)
            pe.wait_ge(s["c_copied"], NB + 1)
            bflat = b_parts[:].rearrange("p q t -> p (q t)")
            pflat = pick[:].rearrange("p s m -> p (s m)")
            pe.sem_inc(s["y_summed"], RING)

            def open_sum(bank, stop=False):
                mm(bank[:], zrow[:, 0:P], zrow[:], start=True, stop=stop)

            def bcast(n0, i, col, sel):
                pe.wait_ge(s["u_b_multiplied"], n0 * 2 + (2 * i + NH))
                mm(b_bc[:], pflat[:, ds(sel, P)], bflat[:, ds(col, L)], start=True, stop=True
                                    ).then_inc(s["b_broadcast"], 1)

            def ysum(n0, i):
                pe.wait_ge(s["product_ready"], n0 + (i + 1 + 2 * CG))
                pe.sem_inc(s["product_claimed"], 1)
                add_to_y(i % RING)

            def add_to_y(slot):
                for r, h in ((0, 0), (1, 1), (0, 1), (1, 0)):
                    q = slice(HP * r, HP * r + HP)
                    ins = mm(y_ps[r][HP * h:HP * h + HP, :], ident[q, q], products[q, slot, h, :],
                             start=False, stop=False, skip_group_check=True)
                ins.then_inc(s["y_summed"], 1)

            def close_sums(b):
                pe.wait_ge(s["end_loaded"], b * (16 * N_END) + 16 * N_END)
                for r in range(2):
                    ins = mm(y_ps[r][:], diagD[:, r, :], silu_x_in[:, r, :], start=False, stop=True)
                ins.then_inc(s["y_complete"], 1)
                mm(ffn_ps[:], b2r_sb[:], gates_in, start=False, stop=False)
                mm(ffn_ps[:], b2s_sb[:], ones_s[:], start=False, stop=True).then_inc(s["experts_complete"], 1)

            def project_out(b):
                pe.wait_ge(s["ffn_sum_ready"], b + 2)
                for r in range(2):
                    pe.wait_ge(s["y_gated"], b * 2 + (r + 1))
                    ins = mm(ffn_ps[:], wout_sb[:, r, :], y_gated[:, r, :], start=(r == 0), stop=(r == 1))
                ins.then_inc(s["attn_projected"], 1)

            def turn_back(b):
                pe.wait_ge(s["product_s_g_ready"], b + 1)
                for j in range(TPB):
                    ins = nc.tensor.transpose(ffn_ps[:, j * P:(j + 1) * P], s_times_g[:, j * P:(j + 1) * P], ident[:])
                ins.then_inc(s["result_turned"], 1)

            W1_AT = {t: (t,) for t in range(HT + 1)}
            W2_AT = {5: (0, 1, 2), 6: (3,), 7: (4,)}

            def group(b, g, t0, last=None, head=False):
                n0 = (b * E + g) * SG
                u = b * E + g
                for i in range(SG):
                    sidx = g * SG + i
                    bcast(n0, i, snap((sidx // SQ) * T + t0), snap((sidx % SQ) * P))
                    for t in W1_AT.get(i, ()):
                        if t == 0:
                            pe.wait_ge(s["w1_loaded"], u * 32 + 32)
                        if t == 1:
                            pe.wait_ge(s["expert_gated"], u + 1)
                        pe.wait_ge(s["gelu_ready"], u * (HT + 1) + (max(t - 1, 0) + 1))
                        src = x_rr if t < HT else x_rs
                        mm(hid_ps[t % 2][:], w1_in[:, t, :], src[:, ds(t0, L)], start=True, stop=True
                                            ).then_inc(s["hidden_made"], 1)
                    if i == HT:
                        pe.wait_ge(s["hidden_made"], (u + 1) * (HT + 1))
                        pe.sem_inc(s["w1_used"], 1)
                    if not head or i >= LAG or last is not None:
                        if head and i == LAG:
                            if last is not None:
                                pe.wait_ge(s["y_gated"], last * 2 + 2)
                            for r in range(2):
                                open_sum(y_ps[r])
                        if i - LAG not in (PAIR, PAIR + 1):
                            ysum(n0, i - LAG)
                    if head and last is not None:
                        if i == LAG - 1:
                            close_sums(last)
                        if i == LAG:
                            project_out(last)
                        if i == SG - 2:
                            turn_back(last)
                    if head and i == SG - 1:
                        if last is not None:
                            pe.wait_ge(s["result_ready"], last + 2)
                        open_sum(ffn_ps)
                    for t in W2_AT.get(i, ()):
                        if t == 0:
                            pe.wait_ge(s["w2_loaded"], u * 32 + 32)
                            pe.wait_ge(s["gelu_ready"], u * (HT + 1) + HT + 1)
                        if t < HT:
                            ins = mm(expert_ps[:], w2_in[:, t, :], hidden[:, t, :], start=(t == 0), stop=(t == HT - 1))
                            if t == HT - 1:
                                ins.then_inc(s["expert_made"], 1)
                        else:
                            pe.wait_ge(s["gelu_ready"], u * (HT + 1) + HT + 2)
                            mm(ffn_ps[:], w2_in[:, t, :], hidden[:, t, :], start=False, stop=False
                                                ).then_inc(s["w2_used"], 1)
                    if i == SG - 2:
                        pe.wait_ge(s["pair_added"], u + 1)
                        pe.sem_inc(s["product_claimed"], 1)
                        add_to_y(RING)

            def run(b, last):
                t0 = snap(b * L)
                group(b, 0, t0, last, head=True)
                with pe.Fori(1, E) as g:
                    group(b, g, t0)
            run(0, None)
            pe.wait_ge(s["b_c_dt_u_stored"], 16 * N_BCDTU * (NB + 1))
            with pe.Fori(1, NB) as b:
                run(b, b - 1)
            for i in range(-LAG, 0):
                ysum(NB * S, i)
            close_sums(NB - 1)
            project_out(NB - 1)
            turn_back(NB - 1)


_INS = ['L0_attn_x', 'L0_attn_norm_w', 'L0_attn_norm_b', 'L0_attn_Win', 'L0_attn_conv_w', 'L0_attn_conv_b',
        'L0_attn_dt_w', 'L0_attn_dt_b', 'L0_attn_A_log', 'L0_attn_D', 'L0_attn_Bp', 'L0_attn_Cp', 'L0_attn_Wout',
        'L0_ffn_g_shared', 'L0_ffn_W1_s', 'L0_ffn_b1_s', 'L0_ffn_W2_s', 'L0_ffn_b2_s', 'L0_ffn_g_routed',
        'L0_ffn_W1_r', 'L0_ffn_b1_r', 'L0_ffn_W2_r', 'L0_ffn_b2_r', 'L0_ffn_centroids']


def kernel(**inputs):
    import numpy as _np
    import concourse.bacc as _bacc
    from concourse import mybir as _mybir
    from concourse.bass_utils import run_bass_kernel_spmd as _run

    nc = _bacc.Bacc("TRN2", target_bir_lowering=False, num_devices=1)
    arrays, args = {}, []
    for name in _INS:
        a = _np.ascontiguousarray(inputs[name])
        arrays[f"in_{name}_dram"] = a
        args.append(nc.dram_tensor(f"in_{name}_dram", a.shape, _mybir.dt.from_np(a.dtype), kind="ExternalInput").ap())
    shape = inputs['L0_attn_x'].shape
    args.append(nc.dram_tensor("out_0_dram", shape, _mybir.dt.float32, kind="ExternalOutput").ap())
    mamba_gated_moe(nc, *args)
    r = _run(nc, [arrays], core_ids=[0])
    return r.results[0]["out_0_dram"]
```
